# Optimizing a Trainium2 kernel written in Bass

```python
import numpy as np
import jax
import jax.numpy as jnp

def _softmax(x, axis=-1):
    return jax.nn.softmax(x, axis=axis)

def _gelu(x):
    return jax.nn.gelu(x, approximate=True)

def _silu(x):
    return jax.nn.silu(x)

def _sigmoid(x):
    return jax.nn.sigmoid(x)

def _layernorm(x, axis=-1, eps=1e-05):
    m = jnp.mean(x, axis=axis, keepdims=True)
    v = jnp.var(x, axis=axis, keepdims=True)
    return (x - m) / jnp.sqrt(v + eps)

def _scatter_add(tgt, idx, src, axis=0):
    return tgt.at[idx].add(src)

def _segment_sum(src, seg, n):
    return jax.ops.segment_sum(src, seg, n)
kernel_name = 'mk_seq_postln_d1_jaxref_r8_f50421'

def setup_inputs(seed: int=0):
    np.random.seed(seed)
    _w = jnp.asarray

    def _L0_attn_setup():
        import jax, jax.numpy as jnp
        import numpy as np
        EMB_DIM = 128
        N_HEADS = 16
        HEAD_DIM = EMB_DIM // N_HEADS
        WINDOW = 128
        B, T = (4, 256)
        key = jax.random.key(seed)
        k1, k2, k3 = jax.random.split(key, 3)
        x = jax.random.normal(k1, (B, T, EMB_DIM), dtype=jnp.float32)
        s1 = 1.0 / np.sqrt(EMB_DIM)
        w_qkv = jax.random.uniform(k2, (3 * EMB_DIM, EMB_DIM), jnp.float32, -s1, s1)
        w_out = jax.random.uniform(k3, (EMB_DIM, EMB_DIM), jnp.float32, -s1, s1)
        return {'x': x, 'w_qkv': w_qkv, 'w_out': w_out}
    _L0_attn_in = _L0_attn_setup()

    def _L0_ffn_setup():
        import jax, jax.numpy as jnp
        import numpy as np
        H = 16
        TOP_K = 2
        EPS = 1e-05

        def _layer_norm(x, g, b):
            m = x.mean(-1, keepdims=True)
            v = ((x - m) ** 2).mean(-1, keepdims=True)
            return (x - m) * jax.lax.rsqrt(v + EPS) * g + b

        def _block(x, ln1_g, ln1_b, ln2_g, ln2_b, w_qkv, w_o, w_gate, w1, b1, w2, b2):
            B, S, D = x.shape
            hd = D // H
            h = _layer_norm(x, ln1_g, ln1_b)
            qkv = h @ w_qkv
            q, k, v = jnp.split(qkv, 3, axis=-1)
            q = q.reshape(B, S, H, hd)
            k = k.reshape(B, S, H, hd)
            v = v.reshape(B, S, H, hd)
            scores = jnp.einsum('bqhd,bkhd->bhqk', q, k) * hd ** (-0.5)
            causal = jnp.tril(jnp.ones((S, S), bool))
            scores = jnp.where(causal, scores, jnp.finfo(scores.dtype).min)
            attn = jax.nn.softmax(scores, axis=-1)
            o = jnp.einsum('bhqk,bkhd->bqhd', attn, v).reshape(B, S, D)
            x_resid = x + o @ w_o
            moe_in = _layer_norm(x_resid, ln2_g, ln2_b)
            N = B * S
            xf = moe_in.reshape(N, D)
            probs = jax.nn.softmax(xf @ w_gate, axis=-1)
            top_w, top_i = jax.lax.top_k(probs, TOP_K)
            top_w = top_w / top_w.sum(-1, keepdims=True)
            E = w1.shape[0]
            out = jnp.zeros_like(xf)
            for e in range(E):
                gate_e = jnp.sum(jnp.where(top_i == e, top_w, 0.0), axis=-1)
                he = jax.nn.gelu(xf @ w1[e] + b1[e])
                out = out + gate_e[:, None] * (he @ w2[e] + b2[e])
            return out.reshape(B, S, D) + x_resid
        key = jax.random.key(seed)
        ks = jax.random.split(key, 12)
        B, S, D, F, E = (8, 64, 128, 512, 8)
        inp = {'x': jax.random.normal(ks[0], (B, S, D), jnp.float32), 'ln1_g': jnp.ones((D,), jnp.float32), 'ln1_b': jnp.zeros((D,), jnp.float32), 'ln2_g': jnp.ones((D,), jnp.float32), 'ln2_b': jnp.zeros((D,), jnp.float32), 'w_qkv': jax.random.normal(ks[1], (D, 3 * D), jnp.float32) * D ** (-0.5), 'w_o': jax.random.normal(ks[2], (D, D), jnp.float32) * D ** (-0.5), 'w_gate': jax.random.normal(ks[3], (D, E), jnp.float32) * D ** (-0.5), 'w1': jax.random.normal(ks[4], (E, D, F), jnp.float32) * D ** (-0.5), 'b1': jnp.zeros((E, F), jnp.float32), 'w2': jax.random.normal(ks[5], (E, F, D), jnp.float32) * F ** (-0.5), 'b2': jnp.zeros((E, D), jnp.float32)}
        return inp
    _L0_ffn_in = _L0_ffn_setup()
    _d = {'L0_attn_x': _L0_attn_in['x'], 'L0_attn_w_qkv': _L0_attn_in['w_qkv'], 'L0_attn_w_out': _L0_attn_in['w_out'], 'L0_ffn_ln1_g': _L0_ffn_in['ln1_g'], 'L0_ffn_ln1_b': _L0_ffn_in['ln1_b'], 'L0_ffn_ln2_g': _L0_ffn_in['ln2_g'], 'L0_ffn_ln2_b': _L0_ffn_in['ln2_b'], 'L0_ffn_w_qkv': _L0_ffn_in['w_qkv'], 'L0_ffn_w_o': _L0_ffn_in['w_o'], 'L0_ffn_w_gate': _L0_ffn_in['w_gate'], 'L0_ffn_w1': _L0_ffn_in['w1'], 'L0_ffn_b1': _L0_ffn_in['b1'], 'L0_ffn_w2': _L0_ffn_in['w2'], 'L0_ffn_b2': _L0_ffn_in['b2']}
    _x0 = _d['L0_attn_x']
    _d['L0_attn_x'] = jax.random.normal(jax.random.fold_in(jax.random.key(seed), 1), (8, 512, 128), dtype=_x0.dtype)
    del _x0
    return _d

def reference(L0_attn_x, L0_attn_w_qkv, L0_attn_w_out, L0_ffn_ln1_g, L0_ffn_ln1_b, L0_ffn_ln2_g, L0_ffn_ln2_b, L0_ffn_w_qkv, L0_ffn_w_o, L0_ffn_w_gate, L0_ffn_w1, L0_ffn_b1, L0_ffn_w2, L0_ffn_b2):

    def _L0_attn_ref(x, w_qkv, w_out):
        import jax, jax.numpy as jnp
        import numpy as np
        EMB_DIM = 128
        N_HEADS = 16
        HEAD_DIM = EMB_DIM // N_HEADS
        WINDOW = 128
        B, T = (4, 256)
        Bs, Ts, C = x.shape
        scale = HEAD_DIM ** (-0.5)
        qkv = x @ w_qkv.T
        qkv = qkv.reshape(Bs, Ts, 3, N_HEADS, HEAD_DIM)
        qkv = jnp.transpose(qkv, (2, 0, 3, 1, 4))
        q, k, v = (qkv[0], qkv[1], qkv[2])
        scores = jnp.einsum('bhtd,bhsd->bhts', q, k) * scale
        i = jnp.arange(Ts)[:, None]
        j = jnp.arange(Ts)[None, :]
        allowed = (j <= i) & (j >= i - WINDOW)
        scores = jnp.where(allowed[None, None], scores, -jnp.inf)
        attn = jax.nn.softmax(scores, axis=-1)
        out = jnp.einsum('bhts,bhsd->bhtd', attn, v)
        out = jnp.transpose(out, (0, 2, 1, 3)).reshape(Bs, Ts, C)
        return out @ w_out.T

    def _L0_ffn_ref(x, ln1_g, ln1_b, ln2_g, ln2_b, w_qkv, w_o, w_gate, w1, b1, w2, b2):
        import jax, jax.numpy as jnp
        import numpy as np
        H = 16
        TOP_K = 2
        EPS = 1e-05

        def _layer_norm(x, g, b):
            m = x.mean(-1, keepdims=True)
            v = ((x - m) ** 2).mean(-1, keepdims=True)
            return (x - m) * jax.lax.rsqrt(v + EPS) * g + b

        def _block(x, ln1_g, ln1_b, ln2_g, ln2_b, w_qkv, w_o, w_gate, w1, b1, w2, b2):
            B, S, D = x.shape
            hd = D // H
            h = _layer_norm(x, ln1_g, ln1_b)
            qkv = h @ w_qkv
            q, k, v = jnp.split(qkv, 3, axis=-1)
            q = q.reshape(B, S, H, hd)
            k = k.reshape(B, S, H, hd)
            v = v.reshape(B, S, H, hd)
            scores = jnp.einsum('bqhd,bkhd->bhqk', q, k) * hd ** (-0.5)
            causal = jnp.tril(jnp.ones((S, S), bool))
            scores = jnp.where(causal, scores, jnp.finfo(scores.dtype).min)
            attn = jax.nn.softmax(scores, axis=-1)
            o = jnp.einsum('bhqk,bkhd->bqhd', attn, v).reshape(B, S, D)
            x_resid = x + o @ w_o
            moe_in = _layer_norm(x_resid, ln2_g, ln2_b)
            N = B * S
            xf = moe_in.reshape(N, D)
            probs = jax.nn.softmax(xf @ w_gate, axis=-1)
            top_w, top_i = jax.lax.top_k(probs, TOP_K)
            top_w = top_w / top_w.sum(-1, keepdims=True)
            E = w1.shape[0]
            out = jnp.zeros_like(xf)
            for e in range(E):
                gate_e = jnp.sum(jnp.where(top_i == e, top_w, 0.0), axis=-1)
                he = jax.nn.gelu(xf @ w1[e] + b1[e])
                out = out + gate_e[:, None] * (he @ w2[e] + b2[e])
            return out.reshape(B, S, D) + x_resid
        return _block(x, ln1_g, ln1_b, ln2_g, ln2_b, w_qkv, w_o, w_gate, w1, b1, w2, b2)
    x = L0_attn_x
    x = _layernorm(x + _L0_attn_ref(x, L0_attn_w_qkv, L0_attn_w_out), axis=-1)
    x = _layernorm(x + _L0_ffn_ref(x, L0_ffn_ln1_g, L0_ffn_ln1_b, L0_ffn_ln2_g, L0_ffn_ln2_b, L0_ffn_w_qkv, L0_ffn_w_o, L0_ffn_w_gate, L0_ffn_w1, L0_ffn_b1, L0_ffn_w2, L0_ffn_b2), axis=-1)
    return x

_drawn_inputs = setup_inputs


def setup_inputs(seed=0):
    import zlib

    import numpy as np

    out = dict(_drawn_inputs(seed))
    spreads = {'L0_ffn_ln1_g': (1.0, 0.2),
     'L0_ffn_ln1_b': (0.0, 0.1),
     'L0_ffn_ln2_g': (1.0, 0.2),
     'L0_ffn_ln2_b': (0.0, 0.1),
     'L0_ffn_b1': (0.0, 0.331),
     'L0_ffn_b2': (0.0, 0.1)}
    factors = {}
    for name, (base, spread) in spreads.items():
        noise = np.random.default_rng([zlib.crc32(name.encode()), seed]).standard_normal(out[name].shape)
        drawn = base * np.exp(spread * noise) if base else spread * noise
        out[name] = jnp.asarray(drawn.astype(out[name].dtype))
    for name, factor in factors.items():
        out[name] = (out[name] * factor).astype(out[name].dtype)
    return out
```

```python
from contextlib import ExitStack

import numpy as np

import concourse.bass as bass
from concourse import mybir

F32 = mybir.dt.float32
BF16 = mybir.dt.bfloat16
U32 = mybir.dt.uint32
ALU = mybir.AluOpType
ACT = mybir.ActivationFunctionType
AX_X = mybir.AxisListType.X

P = 128
B, T, C = 8, 512, 128
NT = T // P
H, HD = 16, 8
SCALE = float(HD) ** -0.5
EPS = 1e-5
E, F = 8, 512
FT = F // P
TOP = 2
NEG = -3e38

LOCAL, CAUSAL = 0, 1
UNITS = 2 * B
GROUP = 4
GROUPS = H // GROUP
VW = 32

Q_PARTS = (0, 0, 0, 1, 1, 2)
K_PARTS = (0, 1, 2, 0, 1, 0)
SLOTS = len(Q_PARTS)
SHIFT_ROW = SLOTS * HD
SHIFT_ROWS = 2
PARTS = 3
QK_DMAS = 2 * SLOTS + 1

CHUNKS = {
    LOCAL: (((0, 0, 256, 0), (1, 128, 256, 256)), ((2, 256, 256, 0), (3, 384, 128, 256))),
    CAUSAL: (((0, 0, 512, 0),), ((1, 128, 384, 0), (3, 384, 128, 384)), ((2, 256, 256, 0),)),
}
STEPS = {layer: GROUPS * len(CHUNKS[layer]) for layer in CHUNKS}
RING = 2 * GROUP


def max_banks(layer):
    out = []
    for i in range(NT):
        first = max(0, i - 1) * P if layer == LOCAL else 0
        keys = (i + 1) * P - first
        heads = T // keys
        out += [(i, h, heads, first, keys) for h in range(0, H, heads)]
    return out


BANKS = {layer: max_banks(layer) for layer in (LOCAL, CAUSAL)}

JOBS = {
    LOCAL: {1: ("v", "t0"), 2: ("t1", "t2", "t3", "h_stats"), 3: ("on", "h"), 4: ("out", "xt"), 5: ("qk", "norm"), 6: ("xf",),
            7: ("shift", "route")},
    CAUSAL: {1: ("v", "t0"), 2: ("t1", "t2", "t3", "h_stats"), 3: ("on", "h"), 4: ("out", "xt"), 5: ("qk", "norm"), 7: ("xf",),
             8: ("route",), 10: ("shift",)},
}
MAX_STEPS = {LOCAL: range(2, 7), CAUSAL: range(2, 10)}

SEGMENTS = [(-2, 0), (-1, 0), (0, 0), (1, 0), (2, 2), (6, 0), (7, 0), (8, 0), (9, 0), (10, 2), (14, 0), (15, 0), (16, 0)]


def floor0(n):
    return max(0, n) if isinstance(n, int) else n


class Iteration:

    def __init__(self, pair, rep):
        self.pair, self.parity, self.rep = pair, rep % 2, rep
        self.layer_now = self.layer(0)
        self.steps = STEPS[self.layer_now]

    def exists(self, off):
        return 0 <= self.rep + off < UNITS

    def layer(self, off):
        return LOCAL if self.rep + off < B else CAUSAL

    def unit(self, off):
        return self.pair * 2 + (self.parity + off)

    def batch(self, off):
        return self.unit(off) - (0 if self.layer(off) == LOCAL else B)

    def slot(self, off):
        return (self.parity + off) % 2

    def same_parity_before(self, off):
        return self.pair + (self.parity + off) // 2

    def before(self, off, local, causal):
        if self.layer(off) == LOCAL:
            return self.unit(off) * local
        return self.batch(off) * causal + B * local

    def jobs(self, step):
        return JOBS[self.layer_now].get(step, ())

    def banks_at(self, step):
        if not self.exists(1) or step not in MAX_STEPS[self.layer_now]:
            return range(0)
        n, steps = len(BANKS[self.layer(1)]), MAX_STEPS[self.layer_now]
        k = step - steps[0]
        return range(n * k // len(steps), n * (k + 1) // len(steps))


def build(nc, x, w_qkv1, w_out1, g1, b1, g2, b2, w_qkv2, w_o2, w_gate, w1, bias1, w2, bias2, out):
    ctx = ExitStack()
    with ctx:
        def sb(name, shape, dt=F32):
            return ctx.enter_context(nc.sbuf_tensor(name, shape, dt))

        def sem(name):
            return ctx.enter_context(nc.semaphore(name))

        tokens = sb("tokens", [P, B, NT, C])
        resid = sb("resid", [P, B, NT, C])
        tokens_t = tokens[:, :, :, :].rearrange("p b t c -> p b (t c)")
        w1_sb = sb("w1_sb", [P, E, F])
        w2_sb = sb("w2_sb", [P, E, FT, C])
        bias2_sb = sb("bias2_sb", [E, C])
        bias1_t = sb("bias1_t", [P, E * FT])
        wq_sb = [sb("wq1_sb", [P, 3 * C]), sb("wq2_sb", [P, 3 * C])]
        wo_sb = [sb("wo1_sb", [P, C]), sb("wo2_sb", [P, C])]
        wg_sb = sb("wg_sb", [P, E])
        norms = sb("norms", [P, 4])
        ident = sb("ident", [P, P])
        ident_b = sb("ident_b", [P, P], BF16)
        mask_b = sb("mask_b", [P, 2, P], BF16)
        ones_b = sb("ones_b", [SHIFT_ROWS, T], BF16)
        expert_ids = sb("expert_ids", [P, NT, E])
        h_in = [sb(f"h_in{i}", [P, NT, C]) for i in range(2)]
        x_t = sb("x_t", [P, T])
        parts = [sb(f"parts_{s}", [P, PARTS, T], BF16) for s in "qk"]
        rest = [sb(f"rest_{s}", [P, T]) for s in "qk"]
        q_st = [sb(f"q_st{i}", [P, H, T], BF16) for i in range(2)]
        k_st = [sb(f"k_st{i}", [P, H, T], BF16) for i in range(2)]
        v_aug = [sb(f"v_aug{i}", [P, NT, H, VW]) for i in range(2)]
        row_max = [sb(f"row_max{i}", [P, NT, H]) for i in range(2)]
        shift_hi = sb("shift_hi", [H, T], BF16)
        shift_lo = sb("shift_lo", [H, T], BF16)
        probs = sb("probs", [P, RING, T])
        o_t = sb("o_t", [P, GROUPS, T])
        inv_sum = sb("inv_sum", [P, H])
        o_norm = sb("o_norm", [P, NT, C])
        o_norm_t = sb("o_norm_t", [P, T])
        y = sb("y", [P, NT, C])
        moe_in = sb("moe_in", [P, NT, C])
        moe_in_t = sb("moe_in_t", [P, T])
        norm_sb = {kind: (sb(f"stats_{kind}", [P, NT, 6]), sb(f"mean_var_{kind}", [P, NT, 2]), sb(f"var_eps_{kind}", [P, NT]),
                          sb(f"rstd_{kind}", [P, NT])) for kind in ("x1", "h", "moe", "final")}
        neg_half = sb("neg_half", [P, NT])
        logits = sb("logits", [P, NT, E])
        top_val = sb("top_val", [P, NT, 8])
        top_idx = sb("top_idx", [P, NT, 8], U32)
        top_idf = sb("top_idf", [P, NT, TOP])
        gap = sb("gap", [P, NT])
        gap_exp = sb("gap_exp", [P, NT])
        gap_sum = sb("gap_sum", [P, NT])
        top_w = sb("top_w", [P, TOP, NT])
        pick = sb("pick", [P, TOP, NT, E])
        gates = sb("gates", [P, B, NT, E])
        gate_now = sb("gate_now", [P, NT, E])
        wq1_raw, wo1_raw, bias1_raw = y[:, 0:3, :], y[:, 3, :], moe_in[0:E * FT, 0, :]
        gate_t = o_norm_t[0:E, :]
        acc = y
        result = moe_in
        hidden = probs

        def bank(name):
            return ctx.enter_context(nc.psum_tensor(name, [P, T], F32))

        score_ps = [bank(f"score_ps{i}") for i in range(2)]
        max_ps = [bank(f"max_ps{i}") for i in range(2)]
        o_ps = [bank(f"o_ps{i}") for i in range(2)]
        misc = [bank(f"misc{i}") for i in range(2)]
        hidden_ps = score_ps + max_ps
        y_ps = o_ps

        scratch = nc.dram_tensor("parts_dram", (2, 2, PARTS, P, T), BF16, kind="Internal").ap()

        attn_w = sem("attn_w")
        moe_w = sem("moe_w")
        tokens_in = sem("tokens_in")
        consts = sem("consts")
        zeroed = sem("zeroed")
        va_cleared = sem("va_cleared")
        pool_zeroed = sem("pool_zeroed")
        ones_in = sem("ones_in")
        setup_ps = sem("setup_ps")
        setup_sb = sem("setup_sb")
        h_loaded = [sem(f"h_loaded{i}") for i in range(2)]
        h_ready = sem("h_ready")
        xt_ps, xt_sb = sem("xt_ps"), sem("xt_sb")
        q_ps, k_ps = sem("q_ps"), sem("k_ps")
        part0 = [sem(f"part0_{s}") for s in "qk"]
        rest_ready = [sem(f"rest_{s}_ready") for s in "qk"]
        part1 = [sem(f"part1_{s}") for s in "qk"]
        part2 = [sem(f"part2_{s}") for s in "qk"]
        stored = [sem(f"stored_{s}") for s in "qk"]
        qk_loaded = [sem(f"qk_loaded{i}") for i in range(2)]
        v_ps, v_ready = sem("v_ps"), sem("v_ready")
        max_filled, max_taken = sem("max_filled"), sem("max_taken")
        maxt_ps = sem("maxt_ps")
        hi_ready, lo_ready = sem("hi_ready"), sem("lo_ready")
        shift_in = [sem(f"shift_in{i}") for i in range(2)]
        scores_ready = sem("scores_ready")
        exp_done = sem("exp_done")
        masked = sem("masked")
        pv_done = sem("pv_done")
        o_copied = sem("o_copied")
        ot_ps, inv_ready, on_ready = sem("ot_ps"), sem("inv_ready"), sem("on_ready")
        ont_ps, ont_sb = sem("ont_ps"), sem("ont_sb")
        proj_ps, y_ready = sem("proj_ps"), sem("y_ready")
        LN = {}
        for kind in ("x1", "h", "moe", "final"):
            LN[kind] = [sem(f"ln_{kind}_{what}") for what in ("stats", "mean", "var", "rstd")]
        x1_ready = sem("x1_ready")
        sum_ready = sem("sum_ready")
        moe_in_ready = sem("moe_in_ready")
        xf_ps, xf_sb, xf_kept = sem("xf_ps"), sem("xf_sb"), sem("xf_kept")
        logits_ps, logits_sb = sem("logits_ps"), sem("logits_sb")
        routed = sem("routed")
        gap_exped = sem("gap_exped")
        gate_now_ready, gate_t_ps, gate_t_sb = sem("gate_now_ready"), sem("gate_t_ps"), sem("gate_t_sb")
        bias2_ps, acc_started = sem("bias2_ps"), sem("acc_started")
        hidden_filled, hidden_ready = sem("hidden_filled"), sem("hidden_ready")
        expert_ps, expert_added = sem("expert_ps"), sem("expert_added")
        result_ready, result_out = sem("result_ready"), sem("result_out")

        ROUTE = ("vals", "idx", "idf", "sum", "w0", "w1", "eq0", "eq1", "p0", "p1", "gates")
        ATTN_LOADS = 16 * 10
        MOE_LOADS = 16 * 3
        STEPS_ALL = B * (STEPS[LOCAL] + STEPS[CAUSAL])
        CHUNKS_ALL = GROUP * STEPS_ALL
        BANKS_ALL = B * (len(BANKS[LOCAL]) + len(BANKS[CAUSAL]))

        def chunks_before(it, off):
            return it.before(off, GROUP * STEPS[LOCAL], GROUP * STEPS[CAUSAL])

        def steps_before(it, off):
            return it.before(off, STEPS[LOCAL], STEPS[CAUSAL])

        def banks_before(it, off):
            return it.before(off, len(BANKS[LOCAL]), len(BANKS[CAUSAL]))

        dve_stands, pool_stands, sp_stands = sem("dve_stands"), sem("pool_stands"), sem("sp_stands")

        def run(eng, iteration):
            for first, pairs in SEGMENTS:
                if not pairs:
                    iteration(Iteration(first // 2, first))
                    continue
                with eng.Fori(first // 2, first // 2 + pairs) as pair:
                    iteration(Iteration(pair, first))
                    iteration(Iteration(pair, first + 1))

        def run_experts(eng, batch_row):
            batch_row(0)
            with eng.Fori(1, B) as b:
                batch_row(b)

        block = ctx.enter_context(nc.Block())

        @block.sync
        def _(sp):
            def load_tokens(it, off):
                p = it.slot(off)
                sp.wait_ge(xt_ps, floor0(it.unit(off - 1)))
                sp.dma_start(h_in[p][:, :, :], x[it.batch(off)].rearrange("(t p) c -> p t c", p=P)).then_inc(h_loaded[p], 16)

            def iteration(it):
                if it.exists(2) and it.layer(2) == LOCAL:
                    load_tokens(it, 2)
                if it.exists(1):
                    p = it.slot(1)
                    sp.wait_ge(stored[0], it.unit(2) * 16)
                    sp.wait_ge(stored[1], it.unit(2) * 16)
                    sp.sem_inc(sp_stands, 1)
                    sp.wait_ge(scores_ready, floor0(chunks_before(it, 0)))
                    for side, stack, which in ((0, q_st[p], Q_PARTS), (1, k_st[p], K_PARTS)):
                        for s, part in enumerate(which):
                            sp.dma_start(stack[s * HD:(s + 1) * HD, :, :],
                                         scratch[p, side, part].rearrange("(h d) t -> d h t", d=HD)).then_inc(qk_loaded[p], 16)
                    sp.dma_start(q_st[p][SHIFT_ROW:SHIFT_ROW + SHIFT_ROWS, :, :],
                                 q_st[p][SHIFT_ROW + SHIFT_ROWS:SHIFT_ROW + 2 * SHIFT_ROWS, :, :]).then_inc(qk_loaded[p], 16)
                if it.exists(2):
                    p = it.slot(2)
                    for side in range(2):
                        sp.wait_ge(part2[side], it.unit(3))
                        sp.wait_ge(qk_loaded[p], floor0(it.same_parity_before(2) * (16 * QK_DMAS)))
                        sp.dma_start(scratch[p, side].rearrange("c r t -> r c t"), parts[side][:, :, :]).then_inc(stored[side], 16)
                if it.exists(1):
                    p = it.slot(1)
                    sp.wait_ge(lo_ready, it.unit(2))
                    sp.wait_ge(qk_loaded[p], (it.same_parity_before(1) + 1) * (16 * QK_DMAS))
                    sp.dma_start(q_st[p][SHIFT_ROW:SHIFT_ROW + 1, :, :], shift_hi[:, :]).then_inc(shift_in[p], 16)
                    sp.dma_start(q_st[p][SHIFT_ROW + 1:SHIFT_ROW + 2, :, :], shift_lo[:, :]).then_inc(shift_in[p], 16)

            sp.wait_ge(consts, 1)
            sp.wait_ge(zeroed, 2)
            sp.wait_ge(pool_zeroed, 2)
            for p in range(2):
                sp.dma_start(k_st[p][SHIFT_ROW:SHIFT_ROW + SHIFT_ROWS, :, :],
                             ones_b[:, :].unsqueeze(1).to_broadcast([SHIFT_ROWS, H, T])).then_inc(ones_in, 16)
            run(sp, iteration)
            def batch_row(b):
                sp.wait_ge(result_ready, b + 1)
                sp.dma_start(out[b].rearrange("(t p) c -> p t c", p=P), result[:, :, :]).then_inc(result_out, 16)

            run_experts(sp, batch_row)
            sp.wait_ge(result_out, 16 * B)

        @block.gpsimd
        def _(pool):
            nc.gpsimd.memset(neg_half[:, :], -0.5)
            nc.gpsimd.memset(ones_b[:, :], 1.0).then_inc(consts, 1)
            nc.gpsimd.memset(ident[:, :], 0.0)
            nc.gpsimd.memset(ident_b[:, :], 0.0)
            nc.gpsimd.memset(mask_b[:, :, :], 0.0).then_inc(consts, 1)
            pool.wait_ge(consts, 2)
            for one in (ident, ident_b):
                nc.gpsimd.affine_select(out=one[:, :], in_=one[:, :], compare_op=ALU.not_equal, fill=1.0, base=0,
                                        pattern=[[-1, P]], channel_multiplier=1)
            nc.gpsimd.affine_select(out=mask_b[:, 0, :], in_=mask_b[:, 0, :], compare_op=ALU.is_ge, fill=NEG, base=0,
                                    pattern=[[1, P]], channel_multiplier=-1)
            nc.gpsimd.affine_select(out=mask_b[:, 1, :], in_=mask_b[:, 1, :], compare_op=ALU.is_ge, fill=NEG, base=0,
                                    pattern=[[-1, P]], channel_multiplier=1)
            nc.gpsimd.iota(expert_ids[:, :, :], pattern=[[0, NT], [1, E]], base=0, channel_multiplier=0,
                           allow_small_or_imprecise_dtypes=True).then_inc(consts, 1)
            for stack in k_st:
                nc.gpsimd.memset(stack[:, :, :].rearrange("p h t -> p (h t)").bitcast(F32), 0.0).then_inc(pool_zeroed, 1)

            def root(kind, n):
                pool.wait_ge(LN[kind][2], n + 1)
                _, _, var_eps, rstd = norm_sb[kind]
                nc.gpsimd.tensor_tensor(rstd[:, :], var_eps[:, :], neg_half[:, :], ALU.pow).then_inc(LN[kind][3], 1)

            def iteration(it):
                types = len(CHUNKS[it.layer_now])
                for k in range(it.steps):
                    if it.exists(0):
                        chunk = CHUNKS[it.layer_now][k % types]
                        own = [col for _, _, _, col in chunk]
                        ahead = [col + P for _, _, n, col in chunk if it.layer_now == LOCAL and n > P]
                        for c in range(GROUP):
                            n = k * GROUP + c
                            pool.wait_ge(exp_done, chunks_before(it, 0) + n + 1)
                            pool.sem_inc(pool_stands, 1)
                            for columns, sign in ((own, 1), (ahead, -1)):
                                if not columns:
                                    continue
                                step = columns[-1] - columns[0] or P
                                view = probs[:, n % RING, columns[0]:columns[-1] + P]
                                if len(columns) > 1:
                                    view = probs[:, n % RING, :].rearrange("p (n q) -> p n q", q=P)[
                                        :, columns[0] // P:columns[-1] // P + 1:step // P, :]
                                    pattern = [[0, len(columns)], [sign, P]]
                                else:
                                    pattern = [[sign, P]]
                                last = nc.gpsimd.affine_select(out=view, in_=view, compare_op=ALU.is_ge, fill=0.0, base=0,
                                                               pattern=pattern, channel_multiplier=-sign)
                            last.then_inc(masked, 1)
                    jobs = it.jobs(k)
                    if "qk" in jobs and it.exists(2):
                        for side in range(2):
                            pool.wait_ge(part1[side], it.unit(3))
                            nc.gpsimd.tensor_tensor(parts[side][:, 2, :], rest[side][:, :], parts[side][:, 1, :],
                                                    ALU.subtract).then_inc(part2[side], 1)
                    if "h_stats" in jobs and it.exists(2) and it.layer(2) == CAUSAL:
                        root("h", it.batch(2))
                    if "out" in jobs and it.exists(-1):
                        root("x1" if it.layer(-1) == LOCAL else "moe", it.batch(-1))
                    if "xf" in jobs and it.exists(-1) and it.layer(-1) == CAUSAL:
                        pool.wait_ge(xf_sb, it.batch(0))
                        nc.gpsimd.tensor_copy(tokens_t[:, it.batch(-1), :], moe_in_t[:, :]).then_inc(xf_kept, 1)

            run(pool, iteration)
            def batch_row(b):
                root("final", b)

            run_experts(pool, batch_row)

        @block.scalar
        def _(act):
            act.dma_start(wq1_raw, w_qkv1.rearrange("(s o) c -> o s c", o=P)).then_inc(attn_w, 16)
            act.dma_start(wo1_raw, w_out1).then_inc(attn_w, 16)
            act.dma_start(bias1_raw, bias1.rearrange("e (f p) -> (e f) p", p=P)).then_inc(attn_w, 16)
            act.dma_start(wq_sb[1][:, :], w_qkv2).then_inc(attn_w, 16)
            act.dma_start(wo_sb[1][:, :], w_o2).then_inc(attn_w, 16)
            act.dma_start(wg_sb[:, :], w_gate).then_inc(attn_w, 16)
            for i, v in enumerate((g1, b1, g2, b2)):
                act.dma_start(norms[:, i:i + 1], v.unsqueeze(1)).then_inc(attn_w, 16)
            act.dma_start(tokens[:, :, :, :].rearrange("p b t c -> p (b t) c"),
                          x.rearrange("b (t p) c -> p (b t) c", p=P)).then_inc(tokens_in, 16)
            act.wait_ge(setup_ps, 2)
            nc.scalar.activation(wq_sb[0][:, :], misc[0][:, 0:3 * C], ACT.Copy)
            nc.scalar.activation(wo_sb[0][:, :], misc[1][:, 0:C], ACT.Copy)
            nc.scalar.activation(bias1_t[:, :], misc[1][:, C:C + E * FT], ACT.Copy).then_inc(setup_sb, 1)
            act.dma_start(w1_sb[:, :, :], w1.rearrange("e d f -> d e f")).then_inc(moe_w, 16)
            act.dma_start(w2_sb[:, :, :, :].rearrange("p e f c -> p (e f) c"),
                          w2.rearrange("e (f p) c -> p (e f) c", p=P)).then_inc(moe_w, 16)
            act.dma_start(bias2_sb[:, :], bias2).then_inc(moe_w, 16)

            def copy_o(it, off, g):
                types = len(CHUNKS[it.layer(off)])
                act.wait_ge(pv_done, steps_before(it, off) + (g + 1) * types)
                act.wait_ge(ot_ps, floor0(it.unit(off) * NT))
                nc.scalar.activation(o_t[:, g, :], o_ps[g % 2][:, :], ACT.Copy).then_inc(o_copied, 1)

            def iteration(it):
                types = len(CHUNKS[it.layer_now])
                for k in range(it.steps):
                    if it.exists(0):
                        width = sum(n for _, _, n, _ in CHUNKS[it.layer_now][k % types])
                        for c in range(GROUP):
                            n = k * GROUP + c
                            act.wait_ge(scores_ready, chunks_before(it, 0) + n + 1)
                            act.wait_ge(pv_done, floor0(steps_before(it, 0) + (k - 1)))
                            nc.scalar.activation(probs[:, n % RING, 0:width], score_ps[n % 2][:, 0:width], ACT.Exp,
                                                 scale=SCALE).then_inc(exp_done, 1)
                    if k == 0 and it.exists(-1):
                        copy_o(it, -1, GROUPS - 1)
                    if k > 0 and k % types == 0 and it.exists(0):
                        copy_o(it, 0, k // types - 1)
                    jobs = it.jobs(k)
                    if "on" in jobs and it.exists(-1):
                        act.wait_ge(ont_ps, it.unit(0))
                        act.wait_ge(proj_ps, floor0(it.unit(-1)))
                        nc.scalar.activation(o_norm_t[:, :], misc[0][:, :], ACT.Copy).then_inc(ont_sb, 1)
                    if "xt" in jobs and it.exists(2):
                        act.wait_ge(xt_ps, it.unit(3))
                        act.wait_ge(v_ps, floor0(it.unit(2)))
                        if it.layer(2) == LOCAL:
                            nc.scalar.activation(x_t[:, :], misc[0][:, :], ACT.Copy).then_inc(xt_sb, 1)
                        else:
                            nc.scalar.activation(x_t[:, :], misc[0][:, :], ACT.Identity, scale=norms[:, 0:1],
                                                 bias=norms[:, 1:2]).then_inc(xt_sb, 1)
                    if "qk" in jobs and it.exists(2):
                        for side, filled, ps in ((0, q_ps, misc[1]), (1, k_ps, misc[0])):
                            act.wait_ge(filled, it.unit(3))
                            act.wait_ge(stored[side], floor0(it.unit(2) * 16))
                            nc.scalar.activation(parts[side][:, 0, :], ps[:, :], ACT.Copy).then_inc(part0[side], 1)
                        for side in range(2):
                            act.wait_ge(rest_ready[side], it.unit(3))
                            nc.scalar.activation(parts[side][:, 1, :], rest[side][:, :], ACT.Copy).then_inc(part1[side], 1)
                    if it.exists(-1) and it.layer(-1) == CAUSAL:
                        if "xf" in jobs:
                            act.wait_ge(xf_ps, it.batch(0))
                            act.wait_ge(xf_kept, floor0(it.batch(-1)))
                            nc.scalar.activation(moe_in_t[:, :], misc[1][:, :], ACT.Identity, scale=norms[:, 2:3],
                                                 bias=norms[:, 3:4]).then_inc(xf_sb, 1)
                        if "route" in jobs:
                            act.wait_ge(routed, it.batch(-1) * len(ROUTE) + 2)
                            nc.scalar.activation(gap_exp[:, :], gap[:, :], ACT.Exp).then_inc(gap_exped, 1)

            run(act, iteration)
            act.wait_ge(pv_done, STEPS_ALL)
            def batch_row(b):
                act.wait_ge(gate_t_ps, b + 1)
                act.wait_ge(bias2_ps, b)
                nc.scalar.activation(gate_t, misc[0][0:E, :], ACT.Copy).then_inc(gate_t_sb, 1)
                for e in range(E):
                    for f in range(FT):
                        n = e * FT + f
                        act.wait_ge(hidden_filled, b * (E * FT) + (n + 1))
                        if e < 2:
                            act.wait_ge(expert_ps, b * E)
                        else:
                            act.wait_ge(expert_ps, b * E + (e - 1))
                        nc.scalar.activation(hidden[:, n % RING, :], hidden_ps[f][:, :], ACT.Gelu_apprx_tanh,
                                             bias=bias1_t[:, n:n + 1]).then_inc(hidden_ready, 1)

            run_experts(act, batch_row)

        @block.vector
        def _(dve):
            for stack in q_st:
                nc.vector.memset(stack[:, :, :].rearrange("p h t -> p (h t)").bitcast(F32), 0.0).then_inc(zeroed, 1)
            for i, va in enumerate(v_aug):
                nc.vector.memset(va[:, :, :, :], 0.0).then_inc(va_cleared, 1)
            for i, va in enumerate(v_aug):
                dve.wait_ge(va_cleared, i + 1)
                nc.vector.memset(va[:, :, :, HD:HD + 1], 1.0).then_inc(zeroed, 1)

            def norm_stats(kind, n, source, ready):
                stats_done, mean_done, var_done, _ = LN[kind]
                stats, mean_var, var_eps, _ = norm_sb[kind]
                dve.wait_ge(ready, n)
                for t in range(NT):
                    last = nc.vector.bn_stats(stats[:, t, :], source[:, t, :])
                last.then_inc(stats_done, 1)
                dve.wait_ge(stats_done, n + 1)
                dve.sem_inc(dve_stands, 1)
                for t in range(NT):
                    last = nc.vector.bn_aggr(mean_var[:, t, :], stats[:, t, :])
                last.then_inc(mean_done, 1)
                dve.wait_ge(mean_done, n + 1)
                nc.vector.tensor_scalar(var_eps[:, :], mean_var[:, :, 1], EPS, None, ALU.add).then_inc(var_done, 1)

            def norm_apply(kind, n, source, target, ready):
                _, mean_var, _, rstd = norm_sb[kind]
                dve.wait_ge(LN[kind][3], n + 1)
                for t in range(NT):
                    last = nc.vector.tensor_scalar(target[:, t, :], source[:, t, :], mean_var[:, t, 0:1], rstd[:, t:t + 1],
                                                   ALU.subtract, ALU.mult)
                last.then_inc(ready, 1)

            def divide(it, t):
                n = it.unit(-1) * NT + t
                o_view = misc[t % 2][:, :].rearrange("p (h w) -> p h w", w=VW)
                dve.wait_ge(on_ready, n)
                dve.wait_ge(ot_ps, n + 1)
                nc.vector.reciprocal(inv_sum[:, :].unsqueeze(2), o_view[:, :, HD:HD + 1]).then_inc(inv_ready, 1)
                dve.wait_ge(inv_ready, n + 1)
                dve.wait_ge(ont_ps, floor0(it.unit(-1)))
                nc.vector.tensor_tensor(o_norm[:, t, :].rearrange("p (h d) -> p h d", d=HD), o_view[:, :, 0:HD],
                                        inv_sum[:, :].unsqueeze(2).to_broadcast([P, H, HD]), ALU.mult).then_inc(on_ready, 1)

            def finish(it):
                dve.wait_ge(proj_ps, it.unit(0))
                b = it.batch(-1)
                proj = misc[1][:, :].rearrange("p (t c) -> p t c", c=C)
                if it.layer(-1) == LOCAL:
                    dve.wait_ge(tokens_in, 16)
                    dve.wait_ge(x1_ready, b)
                    nc.vector.tensor_tensor(y[:, :, :], proj, tokens[:, b, :, :], ALU.add).then_inc(y_ready, 1)
                    dve.wait_ge(y_ready, it.unit(0))
                    norm_stats("x1", b, y, x1_ready)
                else:
                    dve.wait_ge(x1_ready, B)
                    dve.wait_ge(moe_in_ready, b)
                    dve.wait_ge(sum_ready, b)
                    nc.vector.tensor_tensor(y[:, :, :], proj, resid[:, b, :, :], ALU.add).then_inc(y_ready, 1)
                    dve.wait_ge(y_ready, it.unit(0))
                    dve.wait_ge(h_ready, b + 1)
                    nc.vector.tensor_tensor(resid[:, b, :, :], y[:, :, :], resid[:, b, :, :], ALU.add).then_inc(sum_ready, 1)
                    norm_stats("moe", b, y, moe_in_ready)

            def finish_norm(it):
                b = it.batch(-1)
                if it.layer(-1) == LOCAL:
                    norm_apply("x1", b, y, resid[:, b, :, :], x1_ready)
                else:
                    dve.wait_ge(xf_ps, floor0(b))
                    norm_apply("moe", b, y, moe_in, moe_in_ready)

            def route(it):
                b = it.batch(-1)
                done = {name: b * len(ROUTE) + (i + 1) for i, name in enumerate(ROUTE)}
                dve.wait_ge(routed, b * len(ROUTE))
                dve.wait_ge(logits_ps, b + 1)
                nc.vector.tensor_copy(logits[:, :, :].rearrange("p t e -> p (t e)"), misc[1][:, 0:NT * E]).then_inc(logits_sb, 1)
                dve.wait_ge(logits_sb, b + 1)
                dve.sem_inc(dve_stands, 1)
                for t in range(NT):
                    last = nc.vector.max(top_val[:, t, :], logits[:, t, :])
                last.then_inc(routed, 1)
                dve.wait_ge(routed, done["vals"])
                dve.sem_inc(dve_stands, 1)
                for t in range(NT):
                    nc.vector.max_index(top_idx[:, t, :], top_val[:, t, :], logits[:, t, :])
                nc.vector.tensor_tensor(gap[:, :], top_val[:, :, 1], top_val[:, :, 0], ALU.subtract).then_inc(routed, 1)
                dve.wait_ge(routed, done["idx"])
                nc.vector.tensor_copy(top_idf[:, :, :], top_idx[:, :, 0:TOP]).then_inc(routed, 1)
                dve.wait_ge(gap_exped, b + 1)
                nc.vector.tensor_scalar(gap_sum[:, :], gap_exp[:, :], 1.0, None, ALU.add).then_inc(routed, 1)
                dve.wait_ge(routed, done["sum"])
                nc.vector.reciprocal(top_w[:, 0, :], gap_sum[:, :]).then_inc(routed, 1)
                dve.wait_ge(routed, done["w0"])
                nc.vector.tensor_tensor(top_w[:, 1, :], gap_exp[:, :], top_w[:, 0, :], ALU.mult).then_inc(routed, 1)
                dve.wait_ge(routed, done["w1"])
                for r in range(TOP):
                    nc.vector.tensor_tensor(pick[:, r, :, :], expert_ids[:, :, :],
                                            top_idf[:, :, r:r + 1].to_broadcast([P, NT, E]), ALU.is_equal).then_inc(routed, 1)
                dve.wait_ge(routed, done["eq1"])
                for r in range(TOP):
                    nc.vector.tensor_tensor(pick[:, r, :, :], pick[:, r, :, :],
                                            top_w[:, r, :].unsqueeze(2).to_broadcast([P, NT, E]), ALU.mult).then_inc(routed, 1)
                dve.wait_ge(routed, done["p1"])
                nc.vector.tensor_tensor(gates[:, b, :, :], pick[:, 0, :, :], pick[:, 1, :, :], ALU.add).then_inc(routed, 1)

            def iteration(it):
                for k in range(it.steps):
                    for n in it.banks_at(k):
                        i, h, heads, _, keys = BANKS[it.layer(1)][n]
                        p = it.slot(1)
                        dve.wait_ge(max_filled, banks_before(it, 1) + (n + 1))
                        dve.wait_ge(maxt_ps, floor0(it.unit(0)))
                        nc.vector.tensor_reduce(row_max[p][:, i, h:h + heads],
                                                max_ps[n % 2][:, :][:, 0:heads * keys].rearrange("p (h k) -> p h k", k=keys),
                                                AX_X, ALU.max).then_inc(max_taken, 1)
                    jobs = it.jobs(k)
                    if "v" in jobs and it.exists(1):
                        dve.wait_ge(v_ps, it.unit(2))
                        dve.wait_ge(zeroed, 4)
                        dve.wait_ge(pv_done, floor0(steps_before(it, 0)))
                        nc.vector.tensor_copy(v_aug[it.slot(1)][:, :, :, 0:HD].rearrange("p t h d -> p (t h) d"),
                                              misc[1][:, :].rearrange("p (n d) -> p n d", d=HD)).then_inc(v_ready, 1)
                    if it.exists(-1):
                        for t in range(NT):
                            if f"t{t}" in jobs:
                                divide(it, t)
                    if it.exists(2) and it.layer(2) == CAUSAL:
                        b = it.batch(2)
                        if "h_stats" in jobs:
                            dve.wait_ge(x1_ready, b + 1)
                            norm_stats("h", b, resid[:, b, :, :], h_ready)
                        if "h" in jobs:
                            dve.wait_ge(xt_ps, it.unit(1))
                            norm_apply("h", b, resid[:, b, :, :], h_in[it.slot(2)], h_ready)
                    if "norm" in jobs and it.exists(-1):
                        finish_norm(it)
                    if "out" in jobs and it.exists(-1):
                        finish(it)
                    if "qk" in jobs and it.exists(2):
                        for side, ps in ((0, misc[1]), (1, misc[0])):
                            dve.wait_ge(part0[side], it.unit(3))
                            dve.wait_ge(part2[side], floor0(it.unit(2)))
                            nc.vector.tensor_tensor(rest[side][:, :], ps[:, :], parts[side][:, 0, :],
                                                    ALU.subtract).then_inc(rest_ready[side], 1)
                    if "route" in jobs and it.exists(-1) and it.layer(-1) == CAUSAL:
                        route(it)
                    if "shift" in jobs and it.exists(1):
                        p = it.slot(0)
                        dve.wait_ge(maxt_ps, it.unit(2))
                        dve.wait_ge(shift_in[p], floor0((it.same_parity_before(0) + 1) * 32) if it.exists(0) else 0)
                        nc.vector.tensor_scalar(shift_hi[:, :], misc[0][0:H, :], -1.0, None, ALU.mult).then_inc(hi_ready, 1)
                        dve.wait_ge(hi_ready, it.unit(2))
                        nc.vector.scalar_tensor_tensor(out=shift_lo[:, :], in0=misc[0][0:H, :], scalar=-1.0, in1=shift_hi[:, :],
                                                       op0=ALU.mult, op1=ALU.subtract).then_inc(lo_ready, 1)

            run(dve, iteration)
            def batch_row(b):
                dve.wait_ge(routed, (b + 1) * len(ROUTE))
                dve.wait_ge(gate_t_ps, b)
                nc.vector.tensor_copy(gate_now[:, :, :], gates[:, b, :, :]).then_inc(gate_now_ready, 1)
                dve.wait_ge(bias2_ps, b + 1)
                dve.wait_ge(sum_ready, b + 1)
                dve.wait_ge(moe_in_ready, B)
                dve.wait_ge(result_ready, b)
                nc.vector.tensor_tensor(acc[:, :, :], misc[1][:, :].rearrange("p (t c) -> p t c", c=C), resid[:, b, :, :],
                                        ALU.add).then_inc(acc_started, 1)
                dve.wait_ge(acc_started, b + 1)
                dve.wait_ge(gate_now_ready, b + 1)
                for e in range(E):
                    dve.wait_ge(expert_ps, b * E + (e + 1))
                    dve.wait_ge(expert_added, b * E + e)
                    for t in range(NT):
                        last = nc.vector.scalar_tensor_tensor(out=acc[:, t, :], in0=y_ps[e % 2][:, t * C:(t + 1) * C],
                                                              scalar=gate_now[:, t, e:e + 1], in1=acc[:, t, :],
                                                              op0=ALU.mult, op1=ALU.add)
                    last.then_inc(expert_added, 1)
                dve.wait_ge(expert_added, (b + 1) * E)
                dve.wait_ge(result_out, b * 16)
                norm_stats("final", b, acc, result_ready)
                norm_apply("final", b, acc, result, result_ready)

            run_experts(dve, batch_row)

        @block.tensor
        def _(pe):
            pe.wait_ge(consts, 3)
            pe.wait_ge(attn_w, ATTN_LOADS)
            for s in range(3):
                last = nc.tensor.transpose(misc[0][:, s * C:(s + 1) * C], y[:, s, :], ident[:, :])
            last.then_inc(setup_ps, 1)
            nc.tensor.transpose(misc[1][:, 0:C], wo1_raw, ident[:, :])
            nc.tensor.transpose(misc[1][:, C:C + E * FT], bias1_raw, ident[0:E * FT, 0:E * FT]).then_inc(setup_ps, 1)
            pe.wait_ge(setup_sb, 1)

            def score_chunk(it, k, c):
                n = k * GROUP + c
                types = len(CHUNKS[it.layer_now])
                h = (k // types) * GROUP + c
                p = it.slot(0)
                if n == 0:
                    pe.wait_ge(shift_in[p], (it.same_parity_before(0) + 1) * 32)
                pe.wait_ge(exp_done, floor0(chunks_before(it, 0) + (n - 1)))
                for j, q0, width, col in CHUNKS[it.layer_now][k % types]:
                    last = nc.tensor.matmul(score_ps[n % 2][:, col:col + width], k_st[p][:, h, j * P:(j + 1) * P],
                                            q_st[p][:, h, q0:q0 + width], start=True, stop=True)
                last.then_inc(scores_ready, 1)

            def times_v(it, off, k):
                layer = it.layer(off)
                types = len(CHUNKS[layer])
                g, p = k // types, it.slot(off)
                pe.wait_ge(masked, chunks_before(it, off) + (k + 1) * GROUP)
                if k == 0:
                    pe.wait_ge(v_ready, it.unit(off + 1))
                if k % types == 0:
                    pe.wait_ge(o_copied, floor0(it.unit(off) * GROUPS + (g - 1)))
                for j, q0, width, col in CHUNKS[layer][k % types]:
                    for c in range(GROUP):
                        slot = (k * GROUP + c) % RING
                        last = nc.tensor.matmul(o_ps[g % 2][c * VW:(c + 1) * VW, q0:q0 + width], v_aug[p][:, j, g * GROUP + c, :],
                                                probs[:, slot, col:col + width], start=(j == 0), stop=(j == NT - 1),
                                                skip_group_check=True)
                last.then_inc(pv_done, 1)

            def max_bank(it, n):
                layer = it.layer(1)
                i, h0, heads, first, keys = BANKS[layer][n]
                p = it.slot(1)
                if n == 0:
                    pe.wait_ge(qk_loaded[p], (it.same_parity_before(1) + 1) * (16 * QK_DMAS))
                    pe.wait_ge(ones_in, 32)
                pe.wait_ge(max_taken, floor0(banks_before(it, 1) + (n - 1)))
                for m in range(heads):
                    nc.tensor.matmul(max_ps[n % 2][:, m * keys:(m + 1) * keys], q_st[p][:, h0 + m, i * P:(i + 1) * P],
                                     k_st[p][:, h0 + m, first:first + keys], start=True, stop=False)
                    tiles = 2 if layer == LOCAL and i > 0 else 1
                    last = nc.tensor.matmul(max_ps[n % 2][:, (m + 1) * keys - tiles * P:(m + 1) * keys], ident_b[:, :],
                                            mask_b[:, 2 - tiles:2, :].rearrange("p n k -> p (n k)"), start=False, stop=True)
                last.then_inc(max_filled, 1)

            def side_jobs(it, k):
                jobs = it.jobs(k)
                if "v" in jobs and it.exists(1):
                    pe.wait_ge(rest_ready[0], it.unit(2))
                    if it.exists(-2) and it.layer(-2) == CAUSAL:
                        pe.wait_ge(logits_sb, it.batch(-1))
                    pe.wait_ge(xt_sb, it.unit(2))
                    for t in range(NT):
                        last = nc.tensor.matmul(misc[1][:, t * C:(t + 1) * C], x_t[:, t * P:(t + 1) * P],
                                                wq_sb[it.layer(1)][:, 2 * C:3 * C], start=True, stop=True)
                    last.then_inc(v_ps, 1)
                if it.exists(-1):
                    for t in range(NT):
                        if f"t{t}" not in jobs:
                            continue
                        if t == 0:
                            pe.wait_ge(lo_ready, floor0(it.unit(1)) if it.exists(0) else UNITS)
                            pe.wait_ge(o_copied, it.unit(0) * GROUPS)
                        elif t == 1 and it.exists(1):
                            pe.wait_ge(v_ready, it.unit(2))
                        elif t == 1 and it.exists(-2):
                            pe.wait_ge(logits_sb, it.batch(-1))
                        else:
                            pe.wait_ge(on_ready, it.unit(-1) * NT + (t - 1))
                        for g in range(GROUPS):
                            last = nc.tensor.transpose(misc[t % 2][:, g * P:(g + 1) * P], o_t[:, g, t * P:(t + 1) * P], ident[:, :])
                        last.then_inc(ot_ps, 1)
                if "on" in jobs and it.exists(-1):
                    pe.wait_ge(on_ready, it.unit(0) * NT)
                    for t in range(NT):
                        last = nc.tensor.transpose(misc[0][:, t * P:(t + 1) * P], o_norm[:, t, :], ident[:, :])
                    last.then_inc(ont_ps, 1)
                if "out" in jobs and it.exists(-1):
                    pe.wait_ge(ont_sb, it.unit(0))
                    for t in range(NT):
                        last = nc.tensor.matmul(misc[1][:, t * C:(t + 1) * C], o_norm_t[:, t * P:(t + 1) * P],
                                                wo_sb[it.layer(-1)][:, :], start=True, stop=True)
                    last.then_inc(proj_ps, 1)
                if "xt" in jobs and it.exists(2):
                    p = it.slot(2)
                    if it.layer(2) == LOCAL:
                        pe.wait_ge(h_loaded[p], (it.same_parity_before(2) + 1) * 16)
                    else:
                        pe.wait_ge(h_ready, it.batch(3))
                    if it.exists(-1):
                        pe.wait_ge(ont_sb, it.unit(0))
                    elif it.exists(0):
                        pe.wait_ge(lo_ready, it.unit(1))
                    for t in range(NT):
                        last = nc.tensor.transpose(misc[0][:, t * P:(t + 1) * P], h_in[p][:, t, :], ident[:, :])
                    last.then_inc(xt_ps, 1)
                if "qk" in jobs and it.exists(2):
                    pe.wait_ge(xt_sb, it.unit(3))
                    if it.exists(-1):
                        pe.wait_ge(y_ready, it.unit(0))
                    elif it.exists(1):
                        pe.wait_ge(v_ready, it.unit(2))
                    w = wq_sb[it.layer(2)]
                    nc.tensor.matmul(misc[1][:, :], w[:, 0:C], x_t[:, :], start=True, stop=True).then_inc(q_ps, 1)
                    nc.tensor.matmul(misc[0][:, :], w[:, C:2 * C], x_t[:, :], start=True, stop=True).then_inc(k_ps, 1)
                if it.exists(-1) and it.layer(-1) == CAUSAL:
                    if "xf" in jobs:
                        pe.wait_ge(moe_in_ready, it.batch(0))
                        if it.exists(2):
                            pe.wait_ge(rest_ready[0], it.unit(3))
                        for t in range(NT):
                            last = nc.tensor.transpose(misc[1][:, t * P:(t + 1) * P], moe_in[:, t, :], ident[:, :])
                        last.then_inc(xf_ps, 1)
                    if "route" in jobs:
                        pe.wait_ge(xf_sb, it.batch(0))
                        for t in range(NT):
                            last = nc.tensor.matmul(misc[1][:, t * E:(t + 1) * E], moe_in_t[:, t * P:(t + 1) * P], wg_sb[:, :],
                                                    start=True, stop=True)
                        last.then_inc(logits_ps, 1)
                if "shift" in jobs and it.exists(1):
                    pe.wait_ge(max_taken, banks_before(it, 2))
                    if it.exists(2):
                        pe.wait_ge(rest_ready[1], it.unit(3))
                    elif it.exists(-1):
                        pe.wait_ge(ont_sb, it.unit(0))
                    for i in range(NT):
                        last = nc.tensor.transpose(misc[0][0:H, i * P:(i + 1) * P], row_max[it.slot(1)][:, i, :], ident[:, :])
                    last.then_inc(maxt_ps, 1)

            def iteration(it):
                for k in range(it.steps):
                    banks = list(it.banks_at(k))
                    half = len(banks) // 2
                    if it.exists(0):
                        score_chunk(it, k, 0)
                        score_chunk(it, k, 1)
                    for n in banks[:half]:
                        max_bank(it, n)
                    if it.exists(0):
                        score_chunk(it, k, 2)
                    if k == 0 and it.exists(-1):
                        times_v(it, -1, STEPS[it.layer(-1)] - 1)
                    elif k > 0 and it.exists(0):
                        times_v(it, 0, k - 1)
                    if it.exists(0):
                        score_chunk(it, k, 3)
                    for n in banks[half:]:
                        max_bank(it, n)
                    side_jobs(it, k)

            run(pe, iteration)
            pe.wait_ge(exp_done, CHUNKS_ALL)
            pe.wait_ge(max_taken, BANKS_ALL)
            pe.wait_ge(o_copied, UNITS * GROUPS)
            pe.wait_ge(ont_sb, UNITS)
            pe.wait_ge(logits_sb, B)
            pe.wait_ge(xf_kept, B)
            pe.wait_ge(moe_w, MOE_LOADS)
            def batch_row(b):
                def up(e):
                    for f in range(FT):
                        n = e * FT + f
                        if n >= FT:
                            pe.wait_ge(hidden_ready, b * (E * FT) + (n - FT + 1))
                        else:
                            pe.wait_ge(hidden_ready, b * (E * FT))
                        nc.tensor.matmul(hidden_ps[f][:, :], w1_sb[:, e, f * P:(f + 1) * P], tokens_t[:, b, :],
                                         start=True, stop=True).then_inc(hidden_filled, 1)

                def down(e):
                    pe.wait_ge(hidden_ready, b * (E * FT) + (e + 1) * FT)
                    if e >= 2:
                        pe.wait_ge(expert_added, b * E + (e - 1))
                    else:
                        pe.wait_ge(expert_added, b * E)
                    for t in range(NT):
                        for f in range(FT):
                            last = nc.tensor.matmul(y_ps[e % 2][:, t * C:(t + 1) * C],
                                                    hidden[:, (e * FT + f) % RING, t * P:(t + 1) * P], w2_sb[:, e, f, :],
                                                    start=(f == 0), stop=(f == FT - 1))
                    last.then_inc(expert_ps, 1)

                up(0)
                pe.wait_ge(gate_now_ready, b + 1)
                pe.wait_ge(gate_t_sb, b)
                for t in range(NT):
                    last = nc.tensor.transpose(misc[0][0:E, t * P:(t + 1) * P], gate_now[:, t, :], ident[:, :])
                last.then_inc(gate_t_ps, 1)
                up(1)
                pe.wait_ge(gate_t_sb, b + 1)
                pe.wait_ge(acc_started, b)
                for t in range(NT):
                    last = nc.tensor.matmul(misc[1][:, t * C:(t + 1) * C], gate_t[:, t * P:(t + 1) * P], bias2_sb[:, :],
                                            start=True, stop=True)
                last.then_inc(bias2_ps, 1)
                for e in range(E):
                    down(e)
                    if e + 2 < E:
                        up(e + 2)

            run_experts(pe, batch_row)


INPUTS = ["L0_attn_x", "L0_attn_w_qkv", "L0_attn_w_out", "L0_ffn_ln1_g", "L0_ffn_ln1_b", "L0_ffn_ln2_g", "L0_ffn_ln2_b",
          "L0_ffn_w_qkv", "L0_ffn_w_o", "L0_ffn_w_gate", "L0_ffn_w1", "L0_ffn_b1", "L0_ffn_w2", "L0_ffn_b2"]


def kernel(**inputs):
    import concourse.bacc as bacc
    from concourse.bass_utils import run_bass_kernel_spmd

    nc = bacc.Bacc("TRN2", target_bir_lowering=False, num_devices=1)
    arrays, args = {}, []
    for name in INPUTS:
        a = np.ascontiguousarray(inputs[name])
        arrays[f"in_{name}"] = a
        args.append(nc.dram_tensor(f"in_{name}", a.shape, mybir.dt.from_np(a.dtype), kind="ExternalInput").ap())
    args.append(nc.dram_tensor("out_x", (B, T, C), F32, kind="ExternalOutput").ap())
    build(nc, *args)
    r = run_bass_kernel_spmd(nc, [arrays], core_ids=[0])
    return r.results[0]["out_x"]
```

```python
from contextlib import ExitStack

import numpy as np

import concourse.bass as bass
from concourse import mybir

F32 = mybir.dt.float32
BF16 = mybir.dt.bfloat16
U32 = mybir.dt.uint32
I32 = mybir.dt.int32
ALU = mybir.AluOpType
ACT = mybir.ActivationFunctionType
AX_X = mybir.AxisListType.X

P = 128
B, T, C = 8, 512, 128
NT = T // P
H, HD = 16, 8
SCALE = float(HD) ** -0.5
EPS = 1e-5
E, F = 8, 512
FT = F // P
TOP = 2
NEG = -3e38

N = B * T
WEIGHT, PLACE = C, C + 1
ROW = C + 2
CHOICES = TOP * NT
BLK = 2 * P
BLT = BLK // P
BLOCKS = TOP * N // BLK + E
SEG = N + BLK
SEG_BLOCKS = N // BLK
SPARE = BLOCKS - TOP * N // BLK
TABLE_ROWS = E * SEG + SPARE * BLK
DEPTH = 4
PACK_W1, PACK_W2, PACK_B1, PACK_B2 = 0, F, F + FT * C, F + FT * C + FT
PACK = PACK_B2 + C

LOCAL, CAUSAL = 0, 1
UNITS = 2 * B
GROUP = 4
GROUPS = H // GROUP
VW = 16
QUAD = 32

Q_PARTS = (0, 0, 0, 1, 1, 2)
K_PARTS = (0, 1, 2, 0, 1, 0)
SLOTS = len(Q_PARTS)
SHIFT_ROW = SLOTS * HD
SHIFT_ROWS = 2
PARTS = 3
STACK_ROWS = SHIFT_ROW + SHIFT_ROWS

CHUNKS = {
    LOCAL: (((0, 0, 256, 0), (1, 128, 256, 256)), ((2, 256, 256, 0), (3, 384, 128, 256))),
    CAUSAL: (((0, 0, 512, 0),), ((1, 128, 384, 0), (3, 384, 128, 384)), ((2, 256, 256, 0),)),
}
STEPS = {layer: GROUPS * len(CHUNKS[layer]) for layer in CHUNKS}
RING = 2 * GROUP


def max_banks(layer):
    out = []
    for g in range(GROUPS):
        for i in range(NT):
            first = max(0, i - 1) * P if layer == LOCAL else 0
            keys = (i + 1) * P - first
            heads = T // keys
            out += [(i, h, heads, first, keys) for h in range(g * GROUP, (g + 1) * GROUP, heads)]
    return out


BANKS = {layer: max_banks(layer) for layer in (LOCAL, CAUSAL)}

JOBS = {
    LOCAL: {0: ("v",), 1: ("xt",), 2: ("qk",), 3: ("t0", "t1"), 4: ("t2", "t3"), 5: ("on",), 6: ("out", "shift")},
    CAUSAL: {0: ("v",), 1: ("xt",), 2: ("qk",), 3: ("t0", "t1"), 4: ("t2", "t3"), 5: ("on",), 6: ("out",), 8: ("xf",),
             9: ("route", "shift"), 10: ("rank",)},
}
MAX_STEPS = {LOCAL: range(0, 6), CAUSAL: range(0, 9)}

SEGMENTS = [(-2, 0), (-1, 0), (0, 0), (1, 0), (2, 2), (6, 0), (7, 0), (8, 0), (9, 0), (10, 2), (14, 0), (15, 0), (16, 0)]


def floor0(n):
    return max(0, n) if isinstance(n, int) else n


class Iteration:

    def __init__(self, pair, rep):
        self.pair, self.parity, self.rep = pair, rep % 2, rep
        self.layer_now = self.layer(0)
        self.steps = STEPS[self.layer_now]

    def exists(self, off):
        return 0 <= self.rep + off < UNITS

    def layer(self, off):
        return LOCAL if self.rep + off < B else CAUSAL

    def unit(self, off):
        return self.pair * 2 + (self.parity + off)

    def batch(self, off):
        return self.unit(off) - (0 if self.layer(off) == LOCAL else B)

    def slot(self, off):
        return (self.parity + off) % 2

    def same_parity_before(self, off):
        return self.pair + (self.parity + off) // 2

    def before(self, off, local, causal):
        if self.layer(off) == LOCAL:
            return self.unit(off) * local
        return self.batch(off) * causal + B * local

    def jobs(self, step):
        return JOBS[self.layer_now].get(step, ())

    def banks_at(self, step):
        if not self.exists(1) or step not in MAX_STEPS[self.layer_now]:
            return range(0)
        n, steps = len(BANKS[self.layer(1)]), MAX_STEPS[self.layer_now]
        k = step - steps[0]
        return range(n * k // len(steps), n * (k + 1) // len(steps))

    def after(self, step):
        return self.jobs(step - 1)


def build(nc, x, w_qkv1, w_out1, g1, b1, g2, b2, w_qkv2, w_o2, w_gate, w1, bias1, w2, bias2, out):
    ctx = ExitStack()
    with ctx:
        def sb(name, shape, dt=F32):
            return ctx.enter_context(nc.sbuf_tensor(name, shape, dt))

        def sem(name):
            return ctx.enter_context(nc.semaphore(name))

        tokens = sb("tokens", [P, B, NT, C])
        resid = sb("resid", [P, B, NT, C])
        pack = sb("pack", [P, E, PACK])
        wq_sb = [sb("wq1_sb", [P, 3 * C]), sb("wq2_sb", [P, 3 * C])]
        wo_sb = [sb("wo1_sb", [P, C]), sb("wo2_sb", [P, C])]
        wg_sb = sb("wg_sb", [P, E])
        norms = sb("norms", [P, 4])
        ident = sb("ident", [P, P])
        ident_b = sb("ident_b", [P, P], BF16)
        mask_b = sb("mask_b", [P, 2, P], BF16)
        expert_ids = sb("expert_ids", [P, NT, E])
        h_in = [sb(f"h_in{i}", [P, NT, C]) for i in range(2)]
        x_t = sb("x_t", [P, T])
        parts = [sb(f"parts_{s}", [P, PARTS, T], BF16) for s in "qk"]
        rest = [sb(f"rest_{s}", [P, T]) for s in "qk"]
        q_st = [sb(f"q_st{i}", [P, H, T], BF16) for i in range(2)]
        k_st = [sb(f"k_st{i}", [P, H, T], BF16) for i in range(2)]
        v_aug = [sb(f"v_aug{i}", [P, NT, H, VW]) for i in range(2)]
        row_max = [sb(f"row_max{i}", [P, NT, H]) for i in range(2)]
        shift_hi = sb("shift_hi", [H, T], BF16)
        shift_lo = sb("shift_lo", [H, T], BF16)
        probs = sb("probs", [P, RING, T])
        o_t = [sb(f"o_t{i}", [P, GROUPS, T]) for i in range(2)]
        inv_sum = sb("inv_sum", [P, H])
        o_norm = sb("o_norm", [P, NT, C])
        o_norm_t = sb("o_norm_t", [P, T])
        y = o_norm
        rows = sb("rows", [P, TOP, NT, ROW])
        norm_sb = {kind: (sb(f"stats_{kind}", [P, NT, 6]), sb(f"mean_var_{kind}", [P, NT, 2]), sb(f"var_eps_{kind}", [P, NT]),
                          sb(f"rstd_{kind}", [P, NT])) for kind in ("x1", "h", "moe", "final")}
        neg_half = sb("neg_half", [P, NT])
        logits = sb("logits", [P, NT, E])
        top_val = sb("top_val", [P, NT, 8])
        top_idx = sb("top_idx", [P, NT, 8], U32)
        top_idf = sb("top_idf", [P, NT, TOP])
        gap = sb("gap", [P, NT])
        gap_exp = sb("gap_exp", [P, NT])
        gap_sum = sb("gap_sum", [P, NT])
        onehot = sb("onehot", [P, 2 * CHOICES + 1, E], BF16)
        chosen = onehot[:, CHOICES:2 * CHOICES, :]
        tri_b = sb("tri_b", [P, P], BF16)
        square_b = sb("square_b", [P, P], BF16)
        next_row = sb("next_row", [P, E])
        row_of = sb("row_of", [P, CHOICES, E])
        row_f = sb("row_f", [P, CHOICES])
        row_at = sb("row_at", [P, CHOICES], U32)
        places = sb("places", [P, B, TOP, NT], U32)
        spare_row = rows[:, 0, 0, :]
        block_from = sb("block_from", [P, E, SEG_BLOCKS])
        blocks_of = sb("blocks_of", [P, E])
        not_after = sb("not_after", [P, E, E])
        end_block = sb("end_block", [P, E])
        skip_rows = sb("skip_rows", [P, E])
        block_no = sb("block_no", [P, BLOCKS])
        constant_rows = o_t[1][0:SHIFT_ROWS, 0, :].bitcast(BF16)
        ones_b, zeros_b = constant_rows[:, 0:T], constant_rows[:, T:2 * T]
        moe_in_t = o_norm_t
        plan_end = E * SEG_BLOCKS + E * E
        block_expert = rest[1][:, plan_end:plan_end + BLOCKS].bitcast(I32)
        block_row = rest[1][:, plan_end + BLOCKS:plan_end + 2 * BLOCKS].bitcast(I32)
        past = rest[0][:, 0:BLOCKS * E].rearrange("p (n e) -> p n e", e=E)
        block_f = rest[0][:, BLOCKS * E:BLOCKS * (E + 2)].rearrange("p (w n) -> p w n", w=2)
        block_used = rest[1][:, 0:E * SEG_BLOCKS].rearrange("p (e n) -> p e n", e=E)
        end_terms = rest[1][:, E * SEG_BLOCKS:plan_end].rearrange("p (e n) -> p e n", e=E)
        raw = rest[0][:, :].rearrange("p (s c) -> p s c", c=C)
        wq1_raw, wo1_raw, bias1_raw = raw[:, 0:3, :], raw[:, 3, :], rest[1][0:E * FT, 0:C]
        hidden = probs

        def words(stack):
            return stack[:, :, :].rearrange("p h t -> p (h t)").bitcast(F32)

        block_w = [words(k_st[i % 2])[:, i // 2 * PACK:(i // 2 + 1) * PACK] for i in range(DEPTH)]
        block_x = [words(q_st[1])[:, i * BLT * ROW:(i + 1) * BLT * ROW].rearrange("p (t c) -> p t c", c=ROW) for i in range(DEPTH)]
        block_xt = [x_t[:, i * BLK:(i + 1) * BLK] for i in range(2)]
        block_y = [o_norm[:, i * BLT:(i + 1) * BLT, :] for i in range(2)]
        second = words(q_st[0]).rearrange("p (b t c) -> p b t c", b=B, c=C)

        def bank(name):
            return ctx.enter_context(nc.psum_tensor(name, [P, T], F32))

        score_ps = [bank(f"score_ps{i}") for i in range(2)]
        max_ps = [bank(f"max_ps{i}") for i in range(2)]
        o_ps = [bank(f"o_ps{i}") for i in range(2)]
        misc = [bank(f"misc{i}") for i in range(2)]
        hidden_ps = score_ps + max_ps
        y_ps = o_ps

        scratch = nc.dram_tensor("parts_dram", (2, 2, STACK_ROWS, H, T), BF16, kind="Internal").ap()
        table = nc.dram_tensor("rows_dram", (TABLE_ROWS, ROW), F32, kind="Internal").ap()
        outputs = nc.dram_tensor("outputs_dram", (TOP * N, C), F32, kind="Internal").ap()

        attn_w = sem("attn_w")
        moe_w = sem("moe_w")
        tokens_in = sem("tokens_in")
        consts = sem("consts")
        zeroed = sem("zeroed")
        va_cleared = sem("va_cleared")
        pool_zeroed = sem("pool_zeroed")
        shift_rows = sem("shift_rows")
        o_cleared = sem("o_cleared")
        setup_ps = sem("setup_ps")
        setup_sb = sem("setup_sb")
        h_loaded = [sem(f"h_loaded{i}") for i in range(2)]
        h_ready = sem("h_ready")
        xt_ps, xt_sb = sem("xt_ps"), sem("xt_sb")
        q_ps, k_ps = sem("q_ps"), sem("k_ps")
        part0 = [sem(f"part0_{s}") for s in "qk"]
        rest_ready = [sem(f"rest_{s}_ready") for s in "qk"]
        part1 = [sem(f"part1_{s}") for s in "qk"]
        part2 = [sem(f"part2_{s}") for s in "qk"]
        stored = [sem(f"stored_{s}") for s in "qk"]
        qk_loaded = [[sem(f"qk_loaded{i}_{g}") for g in range(GROUPS)] for i in range(2)]
        v_ps, v_ready = sem("v_ps"), sem("v_ready")
        max_filled, max_taken = sem("max_filled"), sem("max_taken")
        maxt_ps = sem("maxt_ps")
        hi_ready, lo_ready = sem("hi_ready"), sem("lo_ready")
        shift_in = [sem(f"shift_in{i}") for i in range(2)]
        scores_ready = sem("scores_ready")
        exp_done = sem("exp_done")
        masked = sem("masked")
        pv_done = sem("pv_done")
        o_copied = sem("o_copied")
        ot_ps, inv_ready, on_ready = sem("ot_ps"), sem("inv_ready"), sem("on_ready")
        ont_ps, ont_sb = sem("ont_ps"), sem("ont_sb")
        proj_ps, y_ready = sem("proj_ps"), sem("y_ready")
        LN = {}
        for kind in ("x1", "h", "moe", "final"):
            LN[kind] = [sem(f"ln_{kind}_{what}") for what in ("stats", "mean", "var", "rstd")]
        x1_ready = sem("x1_ready")
        sum_ready = sem("sum_ready")
        moe_in_ready = sem("moe_in_ready")
        xf_ps, xf_sb = sem("xf_ps"), sem("xf_sb")
        logits_ps, logits_sb = sem("logits_ps"), sem("logits_sb")
        routed = sem("routed")
        gap_exped = sem("gap_exped")
        rows_copied = sem("rows_copied")
        rows_ready = sem("rows_ready")
        ranked = sem("ranked")
        placing = sem("placing")
        spared = sem("spared")
        rows_out = sem("rows_out")
        planning = sem("planning")
        planned = sem("planned")
        w_in = [sem(f"w_in{i}") for i in range(DEPTH)]
        x_in = [sem(f"x_in{i}") for i in range(DEPTH)]
        bx_ps, bx_sb = sem("bx_ps"), sem("bx_sb")
        hidden_filled, hidden_ready = sem("hidden_filled"), sem("hidden_ready")
        block_ps, biased, block_done = sem("block_ps"), sem("biased"), sem("block_done")
        y_out = [sem(f"y_out{i}") for i in range(DEPTH)]
        y_in = sem("y_in")
        pair_sum, final_sum = sem("pair_sum"), sem("final_sum")
        result_ready, result_out = sem("result_ready"), sem("result_out")

        ROUTE = ("vals", "idx", "idf", "eq0", "eq1", "sum", "w0")
        PLACING = ("at", "next", "own", "sum", "rows")
        PAIRS = FT // 2
        ATTN_LOADS = 16 * 10
        MOE_LOADS = 16 * (2 + E)
        STEPS_ALL = B * (STEPS[LOCAL] + STEPS[CAUSAL])
        CHUNKS_ALL = GROUP * STEPS_ALL
        BANKS_ALL = B * (len(BANKS[LOCAL]) + len(BANKS[CAUSAL]))

        def chunks_before(it, off):
            return it.before(off, GROUP * STEPS[LOCAL], GROUP * STEPS[CAUSAL])

        def steps_before(it, off):
            return it.before(off, STEPS[LOCAL], STEPS[CAUSAL])

        def banks_before(it, off):
            return it.before(off, len(BANKS[LOCAL]), len(BANKS[CAUSAL]))

        dve_stands, pool_stands, sp_stands = sem("dve_stands"), sem("pool_stands"), sem("sp_stands")

        def run(eng, iteration):
            for first, pairs in SEGMENTS:
                if not pairs:
                    iteration(Iteration(first // 2, first))
                    continue
                with eng.Fori(first // 2, first // 2 + pairs) as pair:
                    iteration(Iteration(pair, first))
                    iteration(Iteration(pair, first + 1))

        def run_blocks(eng, stage):
            for n in range(DEPTH):
                stage(n, n, 0)
            with eng.Fori(1, BLOCKS // DEPTH) as turn:
                for i in range(DEPTH):
                    stage(turn * DEPTH + i, DEPTH + i, turn)
            for n in range(BLOCKS, BLOCKS + 2):
                stage(n, n, n // DEPTH)

        def run_rows(eng, row):
            row(0, True)
            with eng.Fori(1, B - 1) as b:
                row(b, True)
            row(B - 1, False)

        block = ctx.enter_context(nc.Block())

        @block.sync
        def _(sp):
            def load_tokens(it, off):
                p = it.slot(off)
                sp.wait_ge(xt_ps, floor0(it.unit(off - 1)))
                sp.dma_start(h_in[p][:, :, :], x[it.batch(off)].rearrange("(t p) c -> p t c", p=P)).then_inc(h_loaded[p], 16)

            def store_parts(it, off):
                p = it.slot(off)
                for side, which in ((0, Q_PARTS), (1, K_PARTS)):
                    sp.wait_ge(part2[side], it.unit(off + 1))
                    for g in range(GROUPS):
                        sp.wait_ge(qk_loaded[p][g], floor0(it.same_parity_before(off) * 32))
                    sp.sem_inc(sp_stands, 1)
                    for s, part in enumerate(which):
                        sp.dma_start(scratch[p, side, s * HD:(s + 1) * HD].rearrange("d h t -> h d t"),
                                     parts[side][:, part, :]).then_inc(stored[side], 16)

            def load_group(it, off, g):
                p = it.slot(off)
                for side in range(2):
                    sp.wait_ge(stored[side], it.unit(off + 1) * (16 * SLOTS))
                sp.sem_inc(sp_stands, 1)
                if it.exists(off - 2):
                    types = len(CHUNKS[it.layer(off - 2)])
                    sp.wait_ge(scores_ready, chunks_before(it, off - 2) + (g + 1) * types * GROUP)
                    sp.sem_inc(sp_stands, 1)
                heads = slice(g * GROUP, (g + 1) * GROUP)
                for side, stack in ((0, q_st[p]), (1, k_st[p])):
                    sp.dma_start(stack[0:STACK_ROWS, heads, :], scratch[p, side, :, heads, :]).then_inc(qk_loaded[p][g], 16)

            def write_shift(it, off):
                p = it.slot(off)
                sp.wait_ge(lo_ready, it.unit(off + 1))
                for g in range(GROUPS):
                    sp.wait_ge(qk_loaded[p][g], (it.same_parity_before(off) + 1) * 32)
                sp.dma_start(q_st[p][SHIFT_ROW:SHIFT_ROW + 1, :, :], shift_hi[:, :]).then_inc(shift_in[p], 16)
                sp.dma_start(q_st[p][SHIFT_ROW + 1:SHIFT_ROW + 2, :, :], shift_lo[:, :]).then_inc(shift_in[p], 16)

            def iteration(it):
                if it.exists(2) and it.layer(2) == LOCAL:
                    load_tokens(it, 2)
                if it.exists(2):
                    store_parts(it, 2)
                    for g in range(GROUPS - 1):
                        load_group(it, 2, g)
                if it.exists(1):
                    write_shift(it, 1)
                if it.exists(2):
                    load_group(it, 2, GROUPS - 1)
                if it.exists(0) and it.layer(0) == LOCAL:
                    e = it.unit(0)
                    sp.dma_start(pack[:, e, PACK_W2:PACK_B1].rearrange("p (f c) -> p f c", c=C),
                                 w2[e].rearrange("(f p) c -> p f c", p=P)).then_inc(moe_w, 16)
                    share = table.rearrange("(n p r) c -> n p r c", n=B, p=P)
                    sp.dma_start(share[it.unit(0)], spare_row.unsqueeze(1).to_broadcast([P, TABLE_ROWS // (B * P), ROW])
                                 ).then_inc(spared, 16)

            sp.wait_ge(consts, 1)
            for p in range(2):
                for side, constant in ((0, zeros_b), (1, ones_b)):
                    sp.dma_start(scratch[p, side, SHIFT_ROW:STACK_ROWS],
                                 constant.unsqueeze(1).to_broadcast([SHIFT_ROWS, H, T])).then_inc(shift_rows, 16)
            sp.wait_ge(shift_rows, 64)
            sp.wait_ge(zeroed, 2)
            sp.wait_ge(pool_zeroed, 2)
            sp.wait_ge(consts, 4)
            run(sp, iteration)

            sp.wait_ge(setup_sb, 1)
            sp.wait_ge(moe_w, MOE_LOADS)
            sp.wait_ge(scores_ready, CHUNKS_ALL)
            sp.wait_ge(planned, 1)
            sp.wait_ge(rows_out, B * CHOICES * 16)

            def stage(n, like, turn):
                if like >= BLOCKS:
                    return
                i = like % DEPTH
                if like >= DEPTH:
                    sp.wait_ge(y_out[i], turn * (BLT * 16))
                    sp.sem_inc(sp_stands, 1)
                expert = nc.values_load(block_expert[0:1, bass.ds(n, 1)], engines=[mybir.EngineType.SP], min_val=0, max_val=E - 1)
                first = nc.values_load(block_row[0:1, bass.ds(n, 1)], engines=[mybir.EngineType.SP], min_val=0,
                                       max_val=TABLE_ROWS - BLK)
                sp.dma_start(block_x[i], table[bass.ds(first, BLK), :].rearrange("(t p) c -> p t c", p=P)).then_inc(x_in[i], 16)
                sp.dma_start(block_w[i], pack[:, bass.ds(expert, 1), :].rearrange("p e w -> p (e w)")).then_inc(w_in[i], 16)

            run_blocks(sp, stage)
            for done in y_out:
                sp.wait_ge(done, BLOCKS // DEPTH * BLT * 16)

            def row(b, more):
                by_choice = outputs.rearrange("(r b t p) c -> r b p t c", r=TOP, b=B, p=P)
                sp.wait_ge(y_in, b * 32)
                for r, place in enumerate((tokens, second)):
                    sp.dma_start(place[:, b, :, :], by_choice[r][b]).then_inc(y_in, 16)

            run_rows(sp, row)
            sp.wait_ge(result_out, 16 * B)

        @block.gpsimd
        def _(pool):
            nc.gpsimd.memset(neg_half[:, :], -0.5)
            nc.gpsimd.memset(zeros_b, 0.0)
            nc.gpsimd.memset(ones_b, 1.0).then_inc(consts, 1)
            nc.gpsimd.memset(ident[:, :], 0.0)
            nc.gpsimd.memset(ident_b[:, :], 0.0)
            nc.gpsimd.memset(mask_b[:, :, :], 0.0).then_inc(consts, 1)
            pool.wait_ge(consts, 2)
            for one in (ident, ident_b):
                nc.gpsimd.affine_select(out=one[:, :], in_=one[:, :], compare_op=ALU.not_equal, fill=1.0, base=0,
                                        pattern=[[-1, P]], channel_multiplier=1)
            nc.gpsimd.affine_select(out=mask_b[:, 0, :], in_=mask_b[:, 0, :], compare_op=ALU.is_ge, fill=NEG, base=0,
                                    pattern=[[1, P]], channel_multiplier=-1)
            nc.gpsimd.affine_select(out=mask_b[:, 1, :], in_=mask_b[:, 1, :], compare_op=ALU.is_ge, fill=NEG, base=0,
                                    pattern=[[-1, P]], channel_multiplier=1)
            nc.gpsimd.iota(expert_ids[:, :, :], pattern=[[0, NT], [1, E]], base=0, channel_multiplier=0,
                           allow_small_or_imprecise_dtypes=True).then_inc(consts, 1)
            nc.gpsimd.memset(spare_row[:, 0:PLACE], 0.0)
            nc.gpsimd.iota(spare_row[:, PLACE:ROW].bitcast(U32), pattern=[[0, 1]], base=TOP * N, channel_multiplier=0).then_inc(consts, 1)
            for stack in k_st:
                nc.gpsimd.memset(words(stack), 0.0).then_inc(pool_zeroed, 1)
            nc.gpsimd.memset(onehot[:, :, :], 0.0)
            nc.gpsimd.memset(square_b[:, :], 1.0)
            nc.gpsimd.memset(tri_b[:, :], 1.0)
            nc.gpsimd.memset(not_after[:, :, :], 1.0).then_inc(consts, 1)
            nc.gpsimd.iota(next_row[:, :], pattern=[[SEG, E]], base=0, channel_multiplier=0, allow_small_or_imprecise_dtypes=True)
            nc.gpsimd.iota(block_from[:, :, :], pattern=[[SEG, E], [BLK, SEG_BLOCKS]], base=0, channel_multiplier=0,
                           allow_small_or_imprecise_dtypes=True)
            nc.gpsimd.iota(block_no[:, :], pattern=[[1, BLOCKS]], base=0, channel_multiplier=0,
                           allow_small_or_imprecise_dtypes=True)
            nc.gpsimd.iota(places[:, :, :, :], pattern=[[T, B], [N, TOP], [P, NT]], base=0, channel_multiplier=1)
            pool.wait_ge(consts, 5)
            nc.gpsimd.affine_select(out=tri_b[:, :], in_=tri_b[:, :], compare_op=ALU.is_ge, fill=0.0, base=-1,
                                    pattern=[[1, P]], channel_multiplier=-1)
            nc.gpsimd.affine_select(out=not_after[:, :, :], in_=not_after[:, :, :], compare_op=ALU.is_ge, fill=0.0, base=0,
                                    pattern=[[1, E], [-1, E]], channel_multiplier=0).then_inc(consts, 1)

            def send(b, j):
                if j == 0:
                    pool.wait_ge(placing, (b + 1) * len(PLACING))
                    pool.wait_ge(rows_copied, b + 1)
                    pool.wait_ge(rows_ready, b + 1)
                    pool.wait_ge(spared, B * 16)
                    pool.sem_inc(pool_stands, 1)
                nc.gpsimd.indirect_dma_start(out=table[:, :], out_offset=bass.IndirectOffsetOnAxis(ap=row_at[:, j:j + 1], axis=0),
                                             in_=rows[:, j // NT, j % NT, :], in_offset=None, bounds_check=TABLE_ROWS - 1,
                                             oob_is_err=False).then_inc(rows_out, 16)

            def root(kind, n):
                pool.wait_ge(LN[kind][2], n + 1)
                _, _, var_eps, rstd = norm_sb[kind]
                nc.gpsimd.tensor_tensor(rstd[:, :], var_eps[:, :], neg_half[:, :], ALU.pow).then_inc(LN[kind][3], 1)

            def iteration(it):
                types = len(CHUNKS[it.layer_now])
                for k in range(it.steps):
                    taken = it.after(k)
                    if k == 0 and it.exists(2) and it.layer(2) == CAUSAL:
                        root("h", it.batch(2))
                    if "out" in taken and it.exists(-1):
                        root("x1" if it.layer(-1) == LOCAL else "moe", it.batch(-1))
                    if it.exists(0):
                        chunk = CHUNKS[it.layer_now][k % types]
                        own = [col for _, _, _, col in chunk]
                        ahead = [col + P for _, _, n, col in chunk if it.layer_now == LOCAL and n > P]
                        for c in range(GROUP):
                            n = k * GROUP + c
                            pool.wait_ge(exp_done, chunks_before(it, 0) + n + 1)
                            pool.sem_inc(pool_stands, 1)
                            for columns, sign in ((own, 1), (ahead, -1)):
                                if not columns:
                                    continue
                                step = columns[-1] - columns[0] or P
                                view = probs[:, n % RING, columns[0]:columns[-1] + P]
                                if len(columns) > 1:
                                    view = probs[:, n % RING, :].rearrange("p (n q) -> p n q", q=P)[
                                        :, columns[0] // P:columns[-1] // P + 1:step // P, :]
                                    pattern = [[0, len(columns)], [sign, P]]
                                else:
                                    pattern = [[sign, P]]
                                last = nc.gpsimd.affine_select(out=view, in_=view, compare_op=ALU.is_ge, fill=0.0, base=0,
                                                               pattern=pattern, channel_multiplier=-sign)
                            last.then_inc(masked, 1)
                    if "qk" in it.after(k - 1) and it.exists(2):
                        for side in range(2):
                            pool.wait_ge(part1[side], it.unit(3))
                            nc.gpsimd.tensor_tensor(parts[side][:, 2, :], rest[side][:, :], parts[side][:, 1, :],
                                                    ALU.subtract).then_inc(part2[side], 1)
                    if it.exists(-2) and it.layer(-2) == CAUSAL and k < NT:
                        for r in range(TOP):
                            send(it.batch(-2), k * TOP + r)

            run(pool, iteration)
            for j in range(CHOICES):
                send(B - 1, j)

            def stage(m, like, turn):
                if like < 2:
                    return
                n, i = m - 2, like % 2
                pool.wait_ge(block_done, n + 1)
                pool.sem_inc(pool_stands, 1)
                for t in range(BLT):
                    place = block_x[(like - 2) % DEPTH][:, t, PLACE:ROW].bitcast(U32)
                    nc.gpsimd.indirect_dma_start(out=outputs[:, :], out_offset=bass.IndirectOffsetOnAxis(ap=place, axis=0),
                                                 in_=block_y[i][:, t, :], in_offset=None, bounds_check=TOP * N - 1,
                                                 oob_is_err=False).then_inc(y_out[(like - 2) % DEPTH], 16)

            run_blocks(pool, stage)

            def row(b, more):
                pool.wait_ge(y_in, (b + 1) * 32)
                pool.sem_inc(pool_stands, 1)
                nc.gpsimd.tensor_tensor(tokens[:, b, :, :], tokens[:, b, :, :], second[:, b, :, :], ALU.add).then_inc(pair_sum, 1)
                root("final", b)

            run_rows(pool, row)

        @block.scalar
        def _(act):
            act.dma_start(wq1_raw, w_qkv1.rearrange("(s o) c -> o s c", o=P)).then_inc(attn_w, 16)
            act.dma_start(wo1_raw, w_out1).then_inc(attn_w, 16)
            act.dma_start(bias1_raw, bias1.rearrange("e (f p) -> (e f) p", p=P)).then_inc(attn_w, 16)
            act.dma_start(wq_sb[1][:, :], w_qkv2).then_inc(attn_w, 16)
            act.dma_start(wo_sb[1][:, :], w_o2).then_inc(attn_w, 16)
            act.dma_start(wg_sb[:, :], w_gate).then_inc(attn_w, 16)
            for i, v in enumerate((g1, b1, g2, b2)):
                act.dma_start(norms[:, i:i + 1], v.unsqueeze(1)).then_inc(attn_w, 16)
            act.dma_start(tokens[:, :, :, :].rearrange("p b t c -> p (b t) c"),
                          x.rearrange("b (t p) c -> p (b t) c", p=P)).then_inc(tokens_in, 16)
            act.wait_ge(setup_ps, 2)
            nc.scalar.activation(wq_sb[0][:, :], misc[0][:, 0:3 * C], ACT.Copy)
            nc.scalar.activation(wo_sb[0][:, :], misc[1][:, 0:C], ACT.Copy)
            nc.scalar.activation(pack[:, :, PACK_B1:PACK_B2], misc[1][:, C:C + E * FT].rearrange("p (e f) -> p e f", f=FT),
                                 ACT.Copy).then_inc(setup_sb, 1)
            act.dma_start(pack[:, :, PACK_W1:PACK_W2], w1.rearrange("e d f -> d e f")).then_inc(moe_w, 16)
            act.dma_start(pack[:, :, PACK_B2:PACK], bias2.unsqueeze(0).to_broadcast([P, E, C])).then_inc(moe_w, 16)

            def copy_o(it, off, g):
                types = len(CHUNKS[it.layer(off)])
                act.wait_ge(pv_done, steps_before(it, off) + (g + 1) * types)
                act.wait_ge(ot_ps, floor0(it.unit(off - 1) * NT))
                nc.scalar.activation(o_t[it.slot(off)][:, g, :], o_ps[g % 2][:, :], ACT.Copy).then_inc(o_copied, 1)

            def iteration(it):
                types = len(CHUNKS[it.layer_now])
                for k in range(it.steps):
                    taken = it.after(k)
                    if k == 1 and it.exists(-1):
                        copy_o(it, -1, GROUPS - 1)
                    if k > types and k % types == 1 and it.exists(0):
                        copy_o(it, 0, k // types - 1)
                    if "on" in taken and it.exists(-1):
                        act.wait_ge(ont_ps, it.unit(0))
                        act.wait_ge(proj_ps, floor0(it.unit(-1)))
                        if it.exists(-2) and it.layer(-2) == CAUSAL:
                            act.wait_ge(logits_ps, it.batch(-1))
                        nc.scalar.activation(o_norm_t[:, :], misc[0][:, :], ACT.Copy).then_inc(ont_sb, 1)
                    if "xt" in taken and it.exists(2):
                        act.wait_ge(xt_ps, it.unit(3))
                        act.wait_ge(v_ps, floor0(it.unit(2)))
                        if it.layer(2) == LOCAL:
                            nc.scalar.activation(x_t[:, :], misc[0][:, :], ACT.Copy).then_inc(xt_sb, 1)
                        else:
                            nc.scalar.activation(x_t[:, :], misc[0][:, :], ACT.Identity, scale=norms[:, 0:1],
                                                 bias=norms[:, 1:2]).then_inc(xt_sb, 1)
                    if "qk" in taken and it.exists(2):
                        for side, filled, ps in ((0, q_ps, misc[1]), (1, k_ps, misc[0])):
                            act.wait_ge(filled, it.unit(3))
                            act.wait_ge(stored[side], floor0(it.unit(2) * (16 * SLOTS)))
                            nc.scalar.activation(parts[side][:, 0, :], ps[:, :], ACT.Copy).then_inc(part0[side], 1)
                    if "qk" in it.after(k - 1) and it.exists(2):
                        for side in range(2):
                            act.wait_ge(rest_ready[side], it.unit(3))
                            nc.scalar.activation(parts[side][:, 1, :], rest[side][:, :], ACT.Copy).then_inc(part1[side], 1)
                    if it.exists(-1) and it.layer(-1) == CAUSAL:
                        if "xf" in taken:
                            act.wait_ge(xf_ps, it.batch(0))
                            act.wait_ge(proj_ps, it.unit(0))
                            nc.scalar.activation(moe_in_t[:, :], misc[1][:, :], ACT.Identity, scale=norms[:, 2:3],
                                                 bias=norms[:, 3:4]).then_inc(xf_sb, 1)
                            act.wait_ge(moe_in_ready, it.batch(0))
                            act.wait_ge(rows_out, floor0(it.batch(-1) * (CHOICES * 16)))
                            nc.scalar.activation(rows[:, 1, :, 0:C], rows[:, 0, :, 0:C], ACT.Copy).then_inc(rows_copied, 1)
                        if "route" in it.after(k - 1):
                            act.wait_ge(routed, it.batch(-1) * len(ROUTE) + 2)
                            nc.scalar.activation(gap_exp[:, :], gap[:, :], ACT.Exp).then_inc(gap_exped, 1)
                    if it.exists(0):
                        width = sum(n for _, _, n, _ in CHUNKS[it.layer_now][k % types])
                        for c in range(GROUP):
                            n = k * GROUP + c
                            act.wait_ge(scores_ready, chunks_before(it, 0) + n + 1)
                            act.wait_ge(pv_done, floor0(steps_before(it, 0) + (k - 1)))
                            nc.scalar.activation(probs[:, n % RING, 0:width], score_ps[n % 2][:, 0:width], ACT.Exp,
                                                 scale=SCALE).then_inc(exp_done, 1)

            run(act, iteration)
            act.wait_ge(pv_done, STEPS_ALL)
            act.wait_ge(v_ps, UNITS)

            def stage(m, like, turn):
                if 1 <= like <= BLOCKS:
                    n, i, d = m - 1, (like - 1) % 2, (like - 1) % DEPTH
                    if like >= 3:
                        act.wait_ge(block_ps, n - 1)
                    for f in range(FT):
                        if f % 2 == 0:
                            act.wait_ge(hidden_filled, n * PAIRS + (f // 2 + 1))
                        nc.scalar.activation(hidden[:, i * FT + f, 0:BLK], hidden_ps[2 * i + f // 2][:, f % 2 * BLK:(f % 2 + 1) * BLK],
                                             ACT.Gelu_apprx_tanh, bias=block_w[d][:, PACK_B1 + f:PACK_B1 + f + 1]).then_inc(hidden_ready, 1)
                if like < BLOCKS:
                    act.wait_ge(bx_ps, m + 1)
                    if like >= 2:
                        act.wait_ge(hidden_filled, (m - 1) * PAIRS)
                    nc.scalar.activation(block_xt[like % 2], misc[like % 2][:, 0:BLK], ACT.Identity, scale=norms[:, 2:3],
                                         bias=norms[:, 3:4]).then_inc(bx_sb, 1)

            run_blocks(act, stage)

            def row(b, more):
                act.wait_ge(result_ready, b + 1)
                act.dma_start(out[b].rearrange("(t p) c -> p t c", p=P), tokens[:, b, :, :]).then_inc(result_out, 16)

            run_rows(act, row)

        @block.vector
        def _(dve):
            for stack in q_st:
                nc.vector.memset(stack[:, :, :].rearrange("p h t -> p (h t)").bitcast(F32), 0.0).then_inc(zeroed, 1)
            for i, va in enumerate(v_aug):
                nc.vector.memset(va[:, :, :, :], 0.0).then_inc(va_cleared, 1)
            for i, va in enumerate(v_aug):
                dve.wait_ge(va_cleared, i + 1)
                nc.vector.memset(va[:, :, :, HD:HD + 1], 1.0).then_inc(zeroed, 1)

            def norm_stats(kind, n, source, ready):
                stats_done, mean_done, var_done, _ = LN[kind]
                stats, mean_var, var_eps, _ = norm_sb[kind]
                dve.wait_ge(ready, n)
                for t in range(NT):
                    last = nc.vector.bn_stats(stats[:, t, :], source[:, t, :])
                last.then_inc(stats_done, 1)
                dve.wait_ge(stats_done, n + 1)
                dve.sem_inc(dve_stands, 1)
                for t in range(NT):
                    last = nc.vector.bn_aggr(mean_var[:, t, :], stats[:, t, :])
                last.then_inc(mean_done, 1)
                dve.wait_ge(mean_done, n + 1)
                nc.vector.tensor_scalar(var_eps[:, :], mean_var[:, :, 1], EPS, None, ALU.add).then_inc(var_done, 1)

            def norm_apply(kind, n, source, target, ready):
                _, mean_var, _, rstd = norm_sb[kind]
                dve.wait_ge(LN[kind][3], n + 1)
                for t in range(NT):
                    last = nc.vector.tensor_scalar(target[:, t, :], source[:, t, :], mean_var[:, t, 0:1], rstd[:, t:t + 1],
                                                   ALU.subtract, ALU.mult)
                last.then_inc(ready, 1)

            def divide(it, t):
                n = it.unit(-1) * NT + t
                o_view = misc[t % 2][:, :].rearrange("p (h w) -> p h w", w=QUAD)
                dve.wait_ge(on_ready, n)
                dve.wait_ge(ot_ps, n + 1)
                nc.vector.reciprocal(inv_sum[:, :].unsqueeze(2), o_view[:, :, HD:HD + 1]).then_inc(inv_ready, 1)
                dve.wait_ge(inv_ready, n + 1)
                dve.wait_ge(ont_ps, floor0(it.unit(-1)))
                if it.exists(-2):
                    if it.layer(-2) == LOCAL:
                        dve.wait_ge(x1_ready, it.batch(-1) if it.layer(-1) == LOCAL else B)
                    else:
                        dve.wait_ge(moe_in_ready, it.batch(-1))
                nc.vector.tensor_tensor(o_norm[:, t, :].rearrange("p (h d) -> p h d", d=HD), o_view[:, :, 0:HD],
                                        inv_sum[:, :].unsqueeze(2).to_broadcast([P, H, HD]), ALU.mult).then_inc(on_ready, 1)

            def finish(it):
                dve.wait_ge(proj_ps, it.unit(0))
                b = it.batch(-1)
                proj = misc[1][:, :].rearrange("p (t c) -> p t c", c=C)
                if it.layer(-1) == LOCAL:
                    dve.wait_ge(tokens_in, 16)
                    dve.wait_ge(x1_ready, b)
                    nc.vector.tensor_tensor(y[:, :, :], proj, tokens[:, b, :, :], ALU.add).then_inc(y_ready, 1)
                    dve.wait_ge(y_ready, it.unit(0))
                    norm_stats("x1", b, y, x1_ready)
                else:
                    dve.wait_ge(x1_ready, B)
                    dve.wait_ge(moe_in_ready, b)
                    dve.wait_ge(sum_ready, b)
                    nc.vector.tensor_tensor(y[:, :, :], proj, resid[:, b, :, :], ALU.add).then_inc(y_ready, 1)
                    dve.wait_ge(y_ready, it.unit(0))
                    dve.wait_ge(h_ready, b + 1)
                    nc.vector.tensor_tensor(resid[:, b, :, :], y[:, :, :], resid[:, b, :, :], ALU.add).then_inc(sum_ready, 1)
                    norm_stats("moe", b, y, moe_in_ready)

            def finish_norm(it):
                b = it.batch(-1)
                if it.layer(-1) == LOCAL:
                    norm_apply("x1", b, y, resid[:, b, :, :], x1_ready)
                else:
                    dve.wait_ge(xf_ps, floor0(b))
                    dve.wait_ge(rows_out, floor0(b * (CHOICES * 16)))
                    dve.wait_ge(spared, B * 16)
                    norm_apply("moe", b, y, rows[:, 0, :, 0:C], moe_in_ready)

            def route(it):
                b = it.batch(-1)
                done = {name: b * len(ROUTE) + (i + 1) for i, name in enumerate(ROUTE)}
                dve.wait_ge(routed, b * len(ROUTE))
                dve.wait_ge(logits_ps, b + 1)
                nc.vector.tensor_copy(logits[:, :, :].rearrange("p t e -> p (t e)"), misc[1][:, 0:NT * E]).then_inc(logits_sb, 1)
                dve.wait_ge(logits_sb, b + 1)
                dve.sem_inc(dve_stands, 1)
                for t in range(NT):
                    last = nc.vector.max(top_val[:, t, :], logits[:, t, :])
                last.then_inc(routed, 1)
                dve.wait_ge(routed, done["vals"])
                dve.sem_inc(dve_stands, 1)
                for t in range(NT):
                    nc.vector.max_index(top_idx[:, t, :], top_val[:, t, :], logits[:, t, :])
                nc.vector.tensor_tensor(gap[:, :], top_val[:, :, 1], top_val[:, :, 0], ALU.subtract).then_inc(routed, 1)
                dve.wait_ge(routed, done["idx"])
                nc.vector.tensor_copy(top_idf[:, :, :], top_idx[:, :, 0:TOP]).then_inc(routed, 1)

                dve.wait_ge(routed, done["idf"])
                dve.wait_ge(consts, 6)
                dve.wait_ge(ranked, b)
                dve.wait_ge(placing, b * len(PLACING))
                for r in range(TOP):
                    nc.vector.tensor_tensor(chosen[:, r * NT:(r + 1) * NT, :], expert_ids[:, :, :],
                                            top_idf[:, :, r:r + 1].to_broadcast([P, NT, E]), ALU.is_equal).then_inc(routed, 1)

            def place(it):
                b = it.batch(-1)
                done = {name: b * len(PLACING) + (i + 1) for i, name in enumerate(PLACING)}
                earlier = misc[1][:, 0:(CHOICES + 1) * E].rearrange("p (n e) -> p n e", e=E)
                dve.wait_ge(ranked, b + 1)
                dve.wait_ge(placing, b * len(PLACING))
                nc.vector.tensor_tensor(row_of[:, :, :], earlier[:, 0:CHOICES, :], next_row[:, :].unsqueeze(1).to_broadcast([P, CHOICES, E]),
                                        ALU.add).then_inc(placing, 1)
                dve.wait_ge(placing, done["at"])
                nc.vector.tensor_tensor(next_row[:, :], next_row[:, :], earlier[:, CHOICES, :], ALU.add).then_inc(placing, 1)
                nc.vector.tensor_tensor(row_of[:, :, :], row_of[:, :, :], chosen, ALU.mult).then_inc(placing, 1)
                dve.wait_ge(placing, done["own"])
                nc.vector.tensor_reduce(row_f[:, :], row_of[:, :, :], AX_X, ALU.add).then_inc(placing, 1)
                dve.wait_ge(placing, done["sum"])
                dve.wait_ge(rows_out, b * (CHOICES * 16))
                nc.vector.tensor_copy(row_at[:, :], row_f[:, :]).then_inc(placing, 1)

            def weigh(it):
                b = it.batch(-1)
                done = {name: b * len(ROUTE) + (i + 1) for i, name in enumerate(ROUTE)}
                weight = [rows[:, r, :, WEIGHT:WEIGHT + 1].rearrange("p t c -> p (t c)") for r in range(TOP)]
                dve.wait_ge(gap_exped, b + 1)
                nc.vector.tensor_scalar(gap_sum[:, :], gap_exp[:, :], 1.0, None, ALU.add).then_inc(routed, 1)
                dve.wait_ge(routed, done["sum"])
                nc.vector.reciprocal(weight[0], gap_sum[:, :]).then_inc(routed, 1)
                for r in range(TOP):
                    nc.vector.tensor_copy(rows[:, r, :, PLACE:ROW].bitcast(U32).rearrange("p t c -> p (t c)"), places[:, b, r, :])
                dve.wait_ge(routed, done["w0"])
                nc.vector.tensor_tensor(weight[1], gap_exp[:, :], weight[0], ALU.mult).then_inc(rows_ready, 1)

            def iteration(it):
                for k in range(it.steps):
                    taken = it.after(k)
                    if it.exists(2) and it.layer(2) == CAUSAL:
                        b = it.batch(2)
                        if k == 0:
                            dve.wait_ge(x1_ready, b + 1)
                            norm_stats("h", b, resid[:, b, :, :], h_ready)
                        if k == 1:
                            dve.wait_ge(xt_ps, it.unit(1))
                            norm_apply("h", b, resid[:, b, :, :], h_in[it.slot(2)], h_ready)
                    if "v" in taken and it.exists(1):
                        dve.wait_ge(v_ps, it.unit(2))
                        dve.wait_ge(zeroed, 4)
                        dve.wait_ge(pv_done, floor0(steps_before(it, 0)))
                        nc.vector.tensor_copy(v_aug[it.slot(1)][:, :, :, 0:HD].rearrange("p t h d -> p (t h) d"),
                                              misc[1][:, :].rearrange("p (n d) -> p n d", d=HD)).then_inc(v_ready, 1)
                    if "qk" in taken and it.exists(2):
                        for side, ps in ((0, misc[1]), (1, misc[0])):
                            dve.wait_ge(part0[side], it.unit(3))
                            dve.wait_ge(part2[side], floor0(it.unit(2)))
                            nc.vector.tensor_tensor(rest[side][:, :], ps[:, :], parts[side][:, 0, :],
                                                    ALU.subtract).then_inc(rest_ready[side], 1)
                    if it.exists(-1):
                        for t in range(NT):
                            if f"t{t}" in taken:
                                divide(it, t)
                        if "out" in taken:
                            finish(it)
                    if "shift" in taken and it.exists(1):
                        p = it.slot(0)
                        dve.wait_ge(maxt_ps, it.unit(2))
                        if it.exists(0):
                            dve.wait_ge(shift_in[p], (it.same_parity_before(0) + 1) * 32)
                        nc.vector.tensor_scalar(shift_hi[:, :], misc[0][0:H, :], -1.0, None, ALU.mult).then_inc(hi_ready, 1)
                        dve.wait_ge(hi_ready, it.unit(2))
                        nc.vector.scalar_tensor_tensor(out=shift_lo[:, :], in0=misc[0][0:H, :], scalar=-1.0, in1=shift_hi[:, :],
                                                       op0=ALU.mult, op1=ALU.subtract).then_inc(lo_ready, 1)
                    if it.exists(-1) and it.layer(-1) == CAUSAL:
                        if "route" in taken:
                            route(it)
                        if "rank" in taken:
                            place(it)
                        if "route" in it.after(k - 1):
                            weigh(it)
                    for n in it.banks_at(k):
                        i, h, heads, _, keys = BANKS[it.layer(1)][n]
                        p = it.slot(1)
                        dve.wait_ge(max_filled, banks_before(it, 1) + (n + 1))
                        dve.wait_ge(maxt_ps, floor0(it.unit(0)))
                        nc.vector.tensor_reduce(row_max[p][:, i, h:h + heads],
                                                max_ps[n % 2][:, :][:, 0:heads * keys].rearrange("p (h k) -> p h k", k=keys),
                                                AX_X, ALU.max).then_inc(max_taken, 1)
                    if "out" in taken and it.exists(-1):
                        finish_norm(it)

            run(dve, iteration)

            def plan():
                PLAN = ("used", "blocks", "end_terms", "end", "skip", "past", "expert", "limited", "past_rows", "rows", "first")
                done = {name: i + 1 for i, name in enumerate(PLAN)}
                blocks = [P, BLOCKS, E]
                dve.wait_ge(placing, B * len(PLACING))
                for side in range(2):
                    dve.wait_ge(part2[side], UNITS)
                nc.vector.tensor_tensor(block_used, next_row[:, :].unsqueeze(2).to_broadcast([P, E, SEG_BLOCKS]),
                                        block_from[:, :, :], ALU.is_gt).then_inc(planning, 1)
                dve.wait_ge(planning, done["used"])
                nc.vector.tensor_reduce(blocks_of[:, :], block_used, AX_X, ALU.add).then_inc(planning, 1)
                dve.wait_ge(planning, done["blocks"])
                nc.vector.tensor_tensor(end_terms, blocks_of[:, :].unsqueeze(1).to_broadcast([P, E, E]), not_after[:, :, :],
                                        ALU.mult).then_inc(planning, 1)
                dve.wait_ge(planning, done["end_terms"])
                nc.vector.tensor_reduce(end_block[:, :], end_terms, AX_X, ALU.add).then_inc(planning, 1)
                nc.vector.tensor_scalar(skip_rows[:, :], blocks_of[:, :], -float(BLK), float(SEG), ALU.mult, ALU.add).then_inc(planning, 1)
                dve.wait_ge(planning, done["skip"])
                nc.vector.tensor_tensor(past, block_no[:, :].unsqueeze(2).to_broadcast(blocks),
                                        end_block[:, :].unsqueeze(1).to_broadcast(blocks), ALU.is_ge).then_inc(planning, 1)
                dve.wait_ge(planning, done["past"])
                nc.vector.tensor_reduce(block_f[:, 0, :], past, AX_X, ALU.add).then_inc(planning, 1)
                dve.wait_ge(planning, done["expert"])
                nc.vector.tensor_scalar(block_expert, block_f[:, 0, :], float(E - 1), None, ALU.min).then_inc(planning, 1)
                nc.vector.tensor_tensor(past, past, skip_rows[:, :].unsqueeze(1).to_broadcast(blocks),
                                        ALU.mult).then_inc(planning, 1)
                dve.wait_ge(planning, done["past_rows"])
                nc.vector.tensor_reduce(block_f[:, 1, :], past, AX_X, ALU.add).then_inc(planning, 1)
                dve.wait_ge(planning, done["rows"])
                nc.vector.scalar_tensor_tensor(out=block_row, in0=block_no[:, :], scalar=float(BLK), in1=block_f[:, 1, :],
                                               op0=ALU.mult, op1=ALU.add).then_inc(planned, 1)

            plan()
            dve.wait_ge(ont_ps, UNITS)

            def stage(m, like, turn):
                if like < 2:
                    return
                n, i, d = m - 2, like % 2, (like - 2) % DEPTH
                dve.wait_ge(block_ps, n + 1)
                if like >= 4:
                    dve.wait_ge(y_out[like % DEPTH], turn * (BLT * 16))
                nc.vector.tensor_tensor(block_y[i], y_ps[i][:, 0:BLK].rearrange("p (t c) -> p t c", c=C),
                                        block_w[d][:, PACK_B2:PACK].unsqueeze(1).to_broadcast([P, BLT, C]), ALU.add).then_inc(biased, 1)
                dve.wait_ge(biased, n + 1)
                for t in range(BLT):
                    last = nc.vector.tensor_scalar(block_y[i][:, t, :], block_y[i][:, t, :], block_x[d][:, t, WEIGHT:WEIGHT + 1], None,
                                                   ALU.mult)
                last.then_inc(block_done, 1)

            run_blocks(dve, stage)

            def add(b):
                dve.wait_ge(pair_sum, b + 1)
                nc.vector.tensor_tensor(resid[:, b, :, :], resid[:, b, :, :], tokens[:, b, :, :], ALU.add).then_inc(final_sum, 1)

            def row(b, more):
                dve.wait_ge(final_sum, b + 1)
                norm_stats("final", b, resid[:, b, :, :], result_ready)
                if more:
                    add(b + 1)
                norm_apply("final", b, resid[:, b, :, :], tokens[:, b, :, :], result_ready)

            dve.wait_ge(sum_ready, B)
            add(0)
            run_rows(dve, row)

        @block.tensor
        def _(pe):
            pe.wait_ge(consts, 3)
            pe.wait_ge(attn_w, ATTN_LOADS)
            for s in range(3):
                last = nc.tensor.transpose(misc[0][:, s * C:(s + 1) * C], wq1_raw[:, s, :], ident[:, :])
            last.then_inc(setup_ps, 1)
            nc.tensor.transpose(misc[1][:, 0:C], wo1_raw, ident[:, :])
            nc.tensor.transpose(misc[1][:, C:C + E * FT], bias1_raw, ident[0:E * FT, 0:E * FT]).then_inc(setup_ps, 1)
            pe.wait_ge(zeroed, 2)
            for o in o_ps:
                last = nc.tensor.matmul(o[:, :], q_st[0][:, 0, 0:P], q_st[0][:, 0, :], start=True, stop=True)
            last.then_inc(o_cleared, 1)
            pe.wait_ge(setup_sb, 1)

            def score_chunk(it, k, c):
                n = k * GROUP + c
                types = len(CHUNKS[it.layer_now])
                h = (k // types) * GROUP + c
                p = it.slot(0)
                if n == 0:
                    pe.wait_ge(shift_in[p], (it.same_parity_before(0) + 1) * 32)
                pe.wait_ge(exp_done, floor0(chunks_before(it, 0) + (n - 1)))
                for j, q0, width, col in CHUNKS[it.layer_now][k % types]:
                    last = nc.tensor.matmul(score_ps[n % 2][:, col:col + width], k_st[p][:, h, j * P:(j + 1) * P],
                                            q_st[p][:, h, q0:q0 + width], start=True, stop=True)
                last.then_inc(scores_ready, 1)

            def times_v(it, off, k):
                layer = it.layer(off)
                types = len(CHUNKS[layer])
                g, p = k // types, it.slot(off)
                pe.wait_ge(masked, chunks_before(it, off) + (k + 1) * GROUP)
                if k == 0:
                    pe.wait_ge(v_ready, it.unit(off + 1))
                if k % types == 0:
                    pe.wait_ge(o_copied, floor0(it.unit(off) * GROUPS + (g - 1)))
                for j, q0, width, col in CHUNKS[layer][k % types]:
                    for c in range(GROUP):
                        slot = (k * GROUP + c) % RING
                        last = nc.tensor.matmul(o_ps[g % 2][c * QUAD:c * QUAD + VW, q0:q0 + width], v_aug[p][:, j, g * GROUP + c, :],
                                                probs[:, slot, col:col + width], start=(j == 0), stop=(j == NT - 1),
                                                skip_group_check=True)
                last.then_inc(pv_done, 1)

            def max_bank(it, n):
                layer = it.layer(1)
                i, h0, heads, first, keys = BANKS[layer][n]
                p = it.slot(1)
                if i == 0 and first == 0 and h0 % GROUP == 0:
                    pe.wait_ge(qk_loaded[p][h0 // GROUP], (it.same_parity_before(1) + 1) * 32)
                pe.wait_ge(max_taken, floor0(banks_before(it, 1) + (n - 1)))
                for m in range(heads):
                    nc.tensor.matmul(max_ps[n % 2][:, m * keys:(m + 1) * keys], q_st[p][:, h0 + m, i * P:(i + 1) * P],
                                     k_st[p][:, h0 + m, first:first + keys], start=True, stop=False)
                    tiles = 2 if layer == LOCAL and i > 0 else 1
                    last = nc.tensor.matmul(max_ps[n % 2][:, (m + 1) * keys - tiles * P:(m + 1) * keys], ident_b[:, :],
                                            mask_b[:, 2 - tiles:2, :].rearrange("p n k -> p (n k)"), start=False, stop=True)
                last.then_inc(max_filled, 1)

            def side_jobs(it, k):
                jobs = it.jobs(k)
                if "v" in jobs and it.exists(1):
                    pe.wait_ge(rest_ready[0], it.unit(2))
                    if it.exists(-2):
                        pe.wait_ge(y_ready, it.unit(-1))
                        if it.layer(-2) == CAUSAL:
                            pe.wait_ge(placing, it.batch(-2) * len(PLACING) + 2)
                    pe.wait_ge(xt_sb, it.unit(2))
                    for t in range(NT):
                        last = nc.tensor.matmul(misc[1][:, t * C:(t + 1) * C], x_t[:, t * P:(t + 1) * P],
                                                wq_sb[it.layer(1)][:, 2 * C:3 * C], start=True, stop=True)
                    last.then_inc(v_ps, 1)
                if it.exists(-1):
                    for t in range(NT):
                        if f"t{t}" not in jobs:
                            continue
                        if t == 0:
                            pe.wait_ge(o_copied, it.unit(0) * GROUPS)
                        if t >= 2:
                            pe.wait_ge(on_ready, it.unit(-1) * NT + (t - 1))
                        elif it.exists(2):
                            pe.wait_ge(rest_ready[1 - t], it.unit(3))
                        elif t == 0:
                            pe.wait_ge(lo_ready, it.unit(1) if it.exists(0) else UNITS)
                        elif it.exists(1):
                            pe.wait_ge(v_ready, it.unit(2))
                        else:
                            pe.wait_ge(placing, it.batch(-2) * len(PLACING) + 2)
                        for g in range(GROUPS):
                            last = nc.tensor.transpose(misc[t % 2][:, g * P:(g + 1) * P], o_t[it.slot(-1)][:, g, t * P:(t + 1) * P], ident[:, :])
                        last.then_inc(ot_ps, 1)
                if "on" in jobs and it.exists(-1):
                    pe.wait_ge(on_ready, it.unit(0) * NT)
                    for t in range(NT):
                        last = nc.tensor.transpose(misc[0][:, t * P:(t + 1) * P], o_norm[:, t, :], ident[:, :])
                    last.then_inc(ont_ps, 1)
                if "out" in jobs and it.exists(-1):
                    pe.wait_ge(ont_sb, it.unit(0))
                    for t in range(NT):
                        last = nc.tensor.matmul(misc[1][:, t * C:(t + 1) * C], o_norm_t[:, t * P:(t + 1) * P],
                                                wo_sb[it.layer(-1)][:, :], start=True, stop=True)
                    last.then_inc(proj_ps, 1)
                if "xt" in jobs and it.exists(2):
                    p = it.slot(2)
                    if it.layer(2) == LOCAL:
                        pe.wait_ge(h_loaded[p], (it.same_parity_before(2) + 1) * 16)
                    else:
                        pe.wait_ge(h_ready, it.batch(3))
                    if it.exists(0):
                        pe.wait_ge(lo_ready, it.unit(1))
                    elif it.exists(1):
                        pe.wait_ge(rest_ready[1], it.unit(2))
                    for t in range(NT):
                        last = nc.tensor.transpose(misc[0][:, t * P:(t + 1) * P], h_in[p][:, t, :], ident[:, :])
                    last.then_inc(xt_ps, 1)
                if "qk" in jobs and it.exists(2):
                    pe.wait_ge(xt_sb, it.unit(3))
                    if it.exists(1):
                        pe.wait_ge(v_ready, it.unit(2))
                    w = wq_sb[it.layer(2)]
                    nc.tensor.matmul(misc[1][:, :], w[:, 0:C], x_t[:, :], start=True, stop=True).then_inc(q_ps, 1)
                    nc.tensor.matmul(misc[0][:, :], w[:, C:2 * C], x_t[:, :], start=True, stop=True).then_inc(k_ps, 1)
                if it.exists(-1) and it.layer(-1) == CAUSAL:
                    if "xf" in jobs:
                        pe.wait_ge(moe_in_ready, it.batch(0))
                        for t in range(NT):
                            last = nc.tensor.transpose(misc[1][:, t * P:(t + 1) * P], rows[:, 0, t, 0:C], ident[:, :])
                        last.then_inc(xf_ps, 1)
                    if "route" in jobs:
                        pe.wait_ge(xf_sb, it.batch(0))
                        for t in range(NT):
                            last = nc.tensor.matmul(misc[1][:, t * E:(t + 1) * E], moe_in_t[:, t * P:(t + 1) * P], wg_sb[:, :],
                                                    start=True, stop=True)
                        last.then_inc(logits_ps, 1)
                    if "rank" in jobs:
                        pe.wait_ge(routed, it.batch(-1) * len(ROUTE) + 5)
                        width = CHOICES + 1
                        for d in range(width):
                            shifted = onehot[:, CHOICES - d:CHOICES - d + width, :].rearrange("p n e -> p (n e)")
                            last = nc.tensor.matmul(misc[1][:, 0:width * E], square_b[:, :] if d else tri_b[:, :], shifted,
                                                    start=(d == 0), stop=(d == CHOICES))
                        last.then_inc(ranked, 1)
                if "shift" in jobs and it.exists(1):
                    pe.wait_ge(max_taken, banks_before(it, 2))
                    if it.exists(-1):
                        pe.wait_ge(ont_sb, it.unit(0))
                    elif it.exists(2):
                        pe.wait_ge(rest_ready[1], it.unit(3))
                    for i in range(NT):
                        last = nc.tensor.transpose(misc[0][0:H, i * P:(i + 1) * P], row_max[it.slot(1)][:, i, :], ident[:, :])
                    last.then_inc(maxt_ps, 1)

            def iteration(it):
                for k in range(it.steps):
                    banks = list(it.banks_at(k))
                    half = len(banks) // 2
                    if it.exists(0):
                        score_chunk(it, k, 0)
                        score_chunk(it, k, 1)
                    for n in banks[:half]:
                        max_bank(it, n)
                    if it.exists(0):
                        score_chunk(it, k, 2)
                    if k == 0 and it.exists(-1):
                        times_v(it, -1, STEPS[it.layer(-1)] - 1)
                    elif k > 0 and it.exists(0):
                        times_v(it, 0, k - 1)
                    if it.exists(0):
                        score_chunk(it, k, 3)
                    for n in banks[half:]:
                        max_bank(it, n)
                    side_jobs(it, k)

            run(pe, iteration)
            pe.wait_ge(exp_done, CHUNKS_ALL)
            pe.wait_ge(max_taken, BANKS_ALL)
            pe.wait_ge(o_copied, UNITS * GROUPS)
            pe.wait_ge(ont_sb, UNITS)
            pe.wait_ge(placing, B * len(PLACING))

            def loads(turn, like, off):
                return turn + ((like % DEPTH - off) // DEPTH + 1)

            def stage(m, like, turn):
                if 1 <= like <= BLOCKS:
                    n, i, d = m - 1, (like - 1) % 2, (like - 1) % DEPTH
                    pe.wait_ge(w_in[d], loads(turn, like, 1) * 16)
                    pe.wait_ge(bx_sb, n + 1)
                    if like >= 3:
                        pe.wait_ge(hidden_ready, (n - 1) * FT)
                    for f in range(FT):
                        last = nc.tensor.matmul(hidden_ps[2 * i + f // 2][:, f % 2 * BLK:(f % 2 + 1) * BLK],
                                                block_w[d][:, PACK_W1 + f * P:PACK_W1 + (f + 1) * P], block_xt[i],
                                                start=True, stop=True)
                        if f % 2 == 1:
                            last.then_inc(hidden_filled, 1)
                if like < BLOCKS:
                    pe.wait_ge(x_in[like % DEPTH], loads(turn, like, 0) * 16)
                    if like >= 2:
                        pe.wait_ge(bx_sb, m - 1)
                    for t in range(BLT):
                        last = nc.tensor.transpose(misc[like % 2][:, t * P:(t + 1) * P], block_x[like % DEPTH][:, t, 0:C], ident[:, :])
                    last.then_inc(bx_ps, 1)
                if like >= 2:
                    n, i, d = m - 2, like % 2, (like - 2) % DEPTH
                    pe.wait_ge(hidden_ready, (n + 1) * FT)
                    if like >= 4:
                        pe.wait_ge(biased, n - 1)
                    for t in range(BLT):
                        for f in range(FT):
                            last = nc.tensor.matmul(y_ps[i][:, t * C:(t + 1) * C], hidden[:, i * FT + f, t * P:(t + 1) * P],
                                                    block_w[d][:, PACK_W2 + f * C:PACK_W2 + (f + 1) * C],
                                                    start=(f == 0), stop=(f == FT - 1))
                    last.then_inc(block_ps, 1)

            run_blocks(pe, stage)


INPUTS = ["L0_attn_x", "L0_attn_w_qkv", "L0_attn_w_out", "L0_ffn_ln1_g", "L0_ffn_ln1_b", "L0_ffn_ln2_g", "L0_ffn_ln2_b",
          "L0_ffn_w_qkv", "L0_ffn_w_o", "L0_ffn_w_gate", "L0_ffn_w1", "L0_ffn_b1", "L0_ffn_w2", "L0_ffn_b2"]


def kernel(**inputs):
    import concourse.bacc as bacc
    from concourse.bass_utils import run_bass_kernel_spmd

    nc = bacc.Bacc("TRN2", target_bir_lowering=False, num_devices=1)
    arrays, args = {}, []
    for name in INPUTS:
        a = np.ascontiguousarray(inputs[name])
        arrays[f"in_{name}"] = a
        args.append(nc.dram_tensor(f"in_{name}", a.shape, mybir.dt.from_np(a.dtype), kind="ExternalInput").ap())
    args.append(nc.dram_tensor("out_x", (B, T, C), F32, kind="ExternalOutput").ap())
    build(nc, *args)
    r = run_bass_kernel_spmd(nc, [arrays], core_ids=[0])
    return r.results[0]["out_x"]
```

```python
from contextlib import ExitStack

import numpy as np

import concourse.bass as bass
from concourse import mybir

F32 = mybir.dt.float32
BF16 = mybir.dt.bfloat16
U32 = mybir.dt.uint32
I32 = mybir.dt.int32
ALU = mybir.AluOpType
ACT = mybir.ActivationFunctionType
AX_X = mybir.AxisListType.X

P = 128
B, T, C = 8, 512, 128
NT = T // P
H, HD = 16, 8
SCALE = float(HD) ** -0.5
EPS = 1e-5
E, F = 8, 512
FT = F // P
TOP = 2
NEG = -3e38

N = B * T
WEIGHT, PLACE = C, C + 1
ROW = C + 2
CHOICES = TOP * NT
BLK = 2 * P
BLT = BLK // P
BLOCKS = TOP * N // BLK + E
SEG = N + BLK
SEG_BLOCKS = N // BLK
SPARE = BLOCKS - TOP * N // BLK
TABLE_ROWS = E * SEG + SPARE * BLK
DEPTH = 8
W_DEPTH = 4
PACK_W1, PACK_W2, PACK_B1, PACK_B2 = 0, F, F + FT * C, F + FT * C + FT
PACK = PACK_B2 + C

LOCAL, CAUSAL = 0, 1
UNITS = 2 * B
GROUP = 4
GROUPS = H // GROUP
VW = 16
QUAD = 32
MAX_BANKS = 3

PARTS = 3
Q_SLOTS = (slice(0, 3), slice(3, 6, 2), slice(4, 5))
K_SLOTS = (slice(2, 5), slice(0, 6, 5), slice(1, 2))
SLOTS = 7
STACK_ROWS = SLOTS * HD
SHIFT_ROWS = tuple(d * SLOTS + SLOTS - 1 for d in range(2))

CHUNKS = {
    LOCAL: (((0, 0, 256, 0), (1, 128, 256, 256)), ((2, 256, 256, 0), (3, 384, 128, 256))),
    CAUSAL: (((0, 0, 512, 0),), ((1, 128, 384, 0), (3, 384, 128, 384)), ((2, 256, 256, 0),)),
}
STEPS = {layer: GROUPS * len(CHUNKS[layer]) for layer in CHUNKS}
RING = 2 * GROUP


def max_banks(layer):
    out = []
    for g in range(GROUPS):
        for i in range(NT):
            first = max(0, i - 1) * P if layer == LOCAL else 0
            keys = (i + 1) * P - first
            heads = T // keys
            out += [(i, h, heads, first, keys) for h in range(g * GROUP, (g + 1) * GROUP, heads)]
    return out


BANKS = {layer: max_banks(layer) for layer in (LOCAL, CAUSAL)}

JOBS = {
    LOCAL: {0: ("v",), 1: ("xt",), 2: ("qk",), 3: ("t0", "t1"), 4: ("t2", "t3"), 5: ("on",), 6: ("shift", "out")},
    CAUSAL: {0: ("v",), 1: ("t0", "t1"), 2: ("t2", "t3"), 3: ("on",), 4: ("out",), 5: ("xt",), 6: ("qk",), 8: ("xf",), 9: ("route", "shift"),
             10: ("rank",)},
}
LAG = {LOCAL: 0, CAUSAL: 1}
NORM_STEPS = {
    LOCAL: {0: ("h_stats", "h_root"), 1: ("h_norm",), 6: ("stats",), 7: ("root", "norm")},
    CAUSAL: {3: ("h_stats", "h_root"), 4: ("h_norm",), 5: ("stats", "root"), 6: ("norm",), 11: ("weigh",)},
}
SEND_STEPS = range(0, NT)
MAX_STEPS = {LOCAL: range(0, 6), CAUSAL: range(0, 10)}

SEGMENTS = [(-2, 0), (-1, 0), (0, 0), (1, 0), (2, 2), (6, 0), (7, 0), (8, 0), (9, 0), (10, 2), (14, 0), (15, 0), (16, 0)]


def floor0(n):
    return max(0, n) if isinstance(n, int) else n


class Iteration:

    def __init__(self, pair, rep):
        self.pair, self.parity, self.rep = pair, rep % 2, rep
        self.layer_now = self.layer(0)
        self.steps = STEPS[self.layer_now]

    def exists(self, off):
        return 0 <= self.rep + off < UNITS

    def layer(self, off):
        return LOCAL if self.rep + off < B else CAUSAL

    def unit(self, off):
        return self.pair * 2 + (self.parity + off)

    def batch(self, off):
        return self.unit(off) - (0 if self.layer(off) == LOCAL else B)

    def slot(self, off):
        return (self.parity + off) % 2

    def same_parity_before(self, off):
        return self.pair + (self.parity + off) // 2

    def before(self, off, local, causal):
        if self.layer(off) == LOCAL:
            return self.unit(off) * local
        return self.batch(off) * causal + B * local

    def jobs(self, step):
        return JOBS[self.layer_now].get(step, ())

    def taken(self, step):
        return self.jobs(step - LAG[self.layer_now])

    def norms(self, step):
        return NORM_STEPS[self.layer_now].get(step, ())

    def banks_at(self, step):
        if not self.exists(1) or step not in MAX_STEPS[self.layer_now]:
            return range(0)
        n, steps = len(BANKS[self.layer(1)]), MAX_STEPS[self.layer_now]
        k = step - steps[0]
        return range(n * k // len(steps), n * (k + 1) // len(steps))


def build(nc, x, w_qkv1, w_out1, g1, b1, g2, b2, w_qkv2, w_o2, w_gate, w1, bias1, w2, bias2, out):
    ctx = ExitStack()
    with ctx:
        def sb(name, shape, dt=F32):
            return ctx.enter_context(nc.sbuf_tensor(name, shape, dt))

        def sem(name):
            return ctx.enter_context(nc.semaphore(name))

        tokens = sb("tokens", [P, B, NT, C])
        resid = sb("resid", [P, B, NT, C])
        pack = sb("pack", [P, E, PACK])
        wq_sb = [sb("wq1_sb", [P, 3 * C]), sb("wq2_sb", [P, 3 * C])]
        wo_sb = [sb("wo1_sb", [P, C]), sb("wo2_sb", [P, C])]
        wg_sb = sb("wg_sb", [P, E])
        norms = sb("norms", [P, 4])
        ident = sb("ident", [P, P])
        mask_b = {LOCAL: sb("window_b", [P, 2 * P], BF16), CAUSAL: sb("causal_b", [P, T], BF16)}
        expert_ids = sb("expert_ids", [P, NT, E])
        h_in = [sb(f"h_in{i}", [P, NT, C]) for i in range(2)]
        x_t = sb("x_t", [P, T])
        parts = [sb(f"parts_{s}", [P, PARTS, T], BF16) for s in "qk"]
        rest = [sb(f"rest_{s}", [P, T]) for s in "qk"]
        q_st = [sb(f"q_st{i}", [P, H, T], BF16) for i in range(2)]
        k_st = [sb(f"k_st{i}", [P, H, T], BF16) for i in range(2)]
        v_aug = [sb(f"v_aug{i}", [P, NT, H, VW]) for i in range(2)]
        row_max = [sb(f"row_max{i}", [P, NT, H]) for i in range(2)]
        shift_hi = sb("shift_hi", [H, T], BF16)
        shift_lo = sb("shift_lo", [H, T], BF16)
        probs = sb("probs", [P, RING, T])
        o_t = [sb(f"o_t{i}", [P, GROUPS, T]) for i in range(2)]
        inv_sum = sb("inv_sum", [P, H])
        o_norm = sb("o_norm", [P, NT, C])
        o_norm_t = sb("o_norm_t", [P, T])
        y = o_norm
        rows = sb("rows", [P, TOP, NT, ROW])
        norm_sb = {kind: (sb(f"stats_{kind}", [P, NT, 6]), sb(f"mean_var_{kind}", [P, NT, 2]), sb(f"var_eps_{kind}", [P, NT]),
                          sb(f"rstd_{kind}", [P, NT])) for kind in ("x1", "h", "moe")}
        neg_half = sb("neg_half", [P, NT])
        logits = sb("logits", [P, NT, E])
        top_val = sb("top_val", [P, NT, 8])
        top_idx = sb("top_idx", [P, NT, 8], U32)
        top_idf = sb("top_idf", [P, NT, TOP])
        gap = sb("gap", [P, NT])
        gap_exp = sb("gap_exp", [P, NT])
        gap_sum = sb("gap_sum", [P, NT])
        onehot = sb("onehot", [P, 2 * CHOICES + 1, E], BF16)
        chosen = onehot[:, CHOICES:2 * CHOICES, :]
        tri_b = sb("tri_b", [P, P], BF16)
        square_b = sb("square_b", [P, P], BF16)
        next_row = sb("next_row", [P, E])
        row_of = sb("row_of", [P, CHOICES, E])
        row_f = sb("row_f", [P, CHOICES])
        row_at = sb("row_at", [P, CHOICES], U32)
        places = sb("places", [P, B, TOP, NT], U32)
        spare_row = rows[:, 0, 0, :]
        blocks_of = sb("blocks_of", [P, E])
        end_block = sb("end_block", [P, E])
        skip_rows = sb("skip_rows", [P, E])
        constant_rows = o_t[1][:, 0, :].bitcast(BF16)
        ones_b, zeros_b = constant_rows[:, 0:T], constant_rows[:, T:2 * T]
        moe_in_t = o_norm_t
        plan_end = E * SEG_BLOCKS + E * E
        block_expert = rest[1][:, plan_end:plan_end + BLOCKS].bitcast(I32)
        block_row = rest[1][:, plan_end + BLOCKS:plan_end + 2 * BLOCKS].bitcast(I32)
        plan_words = parts[0][:, :, :].rearrange("p n t -> p (n t)").bitcast(F32)
        block_from = plan_words[:, 0:E * SEG_BLOCKS].rearrange("p (e n) -> p e n", e=E)
        not_after = plan_words[:, E * SEG_BLOCKS:E * SEG_BLOCKS + E * E].rearrange("p (e n) -> p e n", e=E)
        block_no = plan_words[:, E * SEG_BLOCKS + E * E:E * SEG_BLOCKS + E * E + BLOCKS]
        past = rest[0][:, 0:BLOCKS * E].rearrange("p (n e) -> p n e", e=E)
        block_f = rest[0][:, BLOCKS * E:BLOCKS * (E + 2)].rearrange("p (w n) -> p w n", w=2)
        block_used = rest[1][:, 0:E * SEG_BLOCKS].rearrange("p (e n) -> p e n", e=E)
        end_terms = rest[1][:, E * SEG_BLOCKS:plan_end].rearrange("p (e n) -> p e n", e=E)
        raw = rest[0][:, :].rearrange("p (s c) -> p s c", c=C)
        wq1_raw, wo1_raw, bias1_raw = raw[:, 0:3, :], raw[:, 3, :], rest[1][0:E * FT, 0:C]
        hidden = probs

        def words(stack):
            return stack[:, :, :].rearrange("p h t -> p (h t)").bitcast(F32)

        block_w = [words(k_st[i % 2])[:, i // 2 * PACK:(i // 2 + 1) * PACK] for i in range(W_DEPTH)]
        block_x = [words(q_st[1])[:, i * BLT * ROW:(i + 1) * BLT * ROW].rearrange("p (t c) -> p t c", c=ROW) for i in range(DEPTH)]
        block_xt = [x_t[:, i * BLK:(i + 1) * BLK] for i in range(2)]
        block_y = [o_norm[:, i * BLT:(i + 1) * BLT, :] for i in range(2)]
        first_tiles = tokens[:, :, :, :].rearrange("p b t c -> p (b t) c")
        second_tiles = words(q_st[0]).rearrange("p (n c) -> p n c", c=C)
        sum_tiles = resid[:, :, :, :].rearrange("p b t c -> p (b t) c")

        def bank(name):
            return ctx.enter_context(nc.psum_tensor(name, [P, T], F32))

        score_ps = [bank(f"score_ps{i}") for i in range(2)]
        max_ps = [bank(f"max_ps{i}") for i in range(MAX_BANKS)]
        o_ps = bank("o_ps")
        misc = [bank(f"misc{i}") for i in range(2)]
        hidden_ps = score_ps + max_ps[0:2]
        y_ps = [o_ps, max_ps[2]]

        scratch = nc.dram_tensor("parts_dram", (2, 2, H, STACK_ROWS, T), BF16, kind="Internal").ap()
        table = nc.dram_tensor("rows_dram", (TABLE_ROWS, ROW), F32, kind="Internal").ap()
        outputs = nc.dram_tensor("outputs_dram", (TOP * N, C), F32, kind="Internal").ap()

        ROUTE = ("vals", "idx", "idf", "eq0", "eq1", "sum", "w0")
        PLACING = ("at", "next", "own", "sum", "rows")
        PAIRS = FT // 2
        RAW_LOADS = 16 * 3
        ATTN_LOADS = 16 * 7
        FINAL = ("stats", "mean", "var", "negmean")
        SHARES = B // 2
        TILES = B * NT // SHARES
        MOE_LOADS = 16 * (1 + 2 * E)
        STEPS_ALL = B * (STEPS[LOCAL] + STEPS[CAUSAL])
        CHUNKS_ALL = GROUP * STEPS_ALL
        BANKS_ALL = B * (len(BANKS[LOCAL]) + len(BANKS[CAUSAL]))

        raw_w = sem("raw_w")
        attn_w = sem("attn_w")
        moe_w = sem("moe_w")
        tokens_in = sem("tokens_in")
        consts = sem("consts")
        zeroed = sem("zeroed")
        va_cleared = sem("va_cleared")
        pool_zeroed = sem("pool_zeroed")
        shift_rows = sem("shift_rows")
        o_cleared = sem("o_cleared")
        setup_ps = sem("setup_ps")
        setup_sb = sem("setup_sb")
        h_loaded = [sem(f"h_loaded{i}") for i in range(2)]
        h_ready = sem("h_ready")
        xt_ps, xt_sb = sem("xt_ps"), sem("xt_sb")
        q_ps, k_ps = sem("q_ps"), sem("k_ps")
        part0 = [sem(f"part0_{s}") for s in "qk"]
        rest_ready = [sem(f"rest_{s}_ready") for s in "qk"]
        part1 = [sem(f"part1_{s}") for s in "qk"]
        part2 = [sem(f"part2_{s}") for s in "qk"]
        stored = [sem(f"stored_{s}") for s in "qk"]
        qk_loaded = [[sem(f"qk_loaded{i}_{g}") for g in range(GROUPS)] for i in range(2)]
        v_ps, v_ready = sem("v_ps"), sem("v_ready")
        max_filled, max_taken = sem("max_filled"), sem("max_taken")
        maxt_ps = sem("maxt_ps")
        hi_ready, lo_ready = sem("hi_ready"), sem("lo_ready")
        shift_in = [sem(f"shift_in{i}") for i in range(2)]
        scores_ready = sem("scores_ready")
        exp_done = sem("exp_done")
        masked = sem("masked")
        pv_done = sem("pv_done")
        o_copied = sem("o_copied")
        ot_ps, inv_ready, on_ready = sem("ot_ps"), sem("inv_ready"), sem("on_ready")
        ont_ps, ont_sb = sem("ont_ps"), sem("ont_sb")
        proj_ps, y_ready = sem("proj_ps"), sem("y_ready")
        LN = {}
        for kind in ("x1", "h", "moe"):
            LN[kind] = [sem(f"ln_{kind}_{what}") for what in ("stats", "mean", "var", "rstd")]
        x1_ready = sem("x1_ready")
        sum_ready = sem("sum_ready")
        moe_in_ready = sem("moe_in_ready")
        xf_ps, xf_sb = sem("xf_ps"), sem("xf_sb")
        logits_ps, logits_sb = sem("logits_ps"), sem("logits_sb")
        routed = sem("routed")
        gap_exped = sem("gap_exped")
        rows_copied = sem("rows_copied")
        rows_ready = sem("rows_ready")
        ranked = sem("ranked")
        placing = sem("placing")
        spared = sem("spared")
        rows_out = sem("rows_out")
        planning = sem("planning")
        plan_consts = sem("plan_consts")
        planned = sem("planned")
        w_in = [sem(f"w_in{i}") for i in range(W_DEPTH)]
        x_in = [sem(f"x_in{i}") for i in range(DEPTH)]
        bx_ps, bx_sb = sem("bx_ps"), sem("bx_sb")
        hidden_filled, hidden_ready = sem("hidden_filled"), sem("hidden_ready")
        block_ps, biased, block_done = sem("block_ps"), sem("biased"), sem("block_done")
        y_out = [sem(f"y_out{i}") for i in range(DEPTH)]
        y_in = [sem(f"y_in{i}") for i in range(SHARES)]
        halves_ready = sem("halves_ready")
        pair_sum, final_sum = sem("pair_sum"), sem("final_sum")
        final_done = sem("final_done")
        final_root, centred = sem("final_root"), sem("centred")
        result_ready, result_out = sem("result_ready"), sem("result_out")

        def chunks_before(it, off):
            return it.before(off, GROUP * STEPS[LOCAL], GROUP * STEPS[CAUSAL])

        def steps_before(it, off):
            return it.before(off, STEPS[LOCAL], STEPS[CAUSAL])

        def banks_before(it, off):
            return it.before(off, len(BANKS[LOCAL]), len(BANKS[CAUSAL]))

        dve_stands, pool_stands, sp_stands = sem("dve_stands"), sem("pool_stands"), sem("sp_stands")

        def run(eng, iteration):
            for first, pairs in SEGMENTS:
                if not pairs:
                    iteration(Iteration(first // 2, first))
                    continue
                with eng.Fori(first // 2, first // 2 + pairs) as pair:
                    iteration(Iteration(pair, first))
                    iteration(Iteration(pair, first + 1))

        def loads(turn, like, off, depth=DEPTH):
            return turn * (DEPTH // depth) + ((like % DEPTH - off) // depth + 1)

        def run_blocks(eng, stage):
            for n in range(DEPTH):
                stage(n, n, 0)
            with eng.Fori(1, BLOCKS // DEPTH) as turn:
                for i in range(DEPTH):
                    stage(turn * DEPTH + i, DEPTH + i, turn)
            for n in range(BLOCKS, BLOCKS + 2):
                stage(n, n, n // DEPTH)

        def tiles(share):
            return slice(share * TILES, (share + 1) * TILES)

        final_sb = v_aug[0][:, :, :, :].rearrange("p t h d -> p (t h d)")

        def final(n, width):
            return final_sb[:, n * B * NT:(n + width) * B * NT].rearrange("p (t w) -> p t w", w=width)

        final_stats, final_mean, final_var, final_rstd, final_negmean = final(0, 6), final(6, 2), final(8, 1), final(9, 1), final(10, 1)
        halves = final(11, 1)

        block = ctx.enter_context(nc.Block())

        @block.sync
        def _(sp):
            def by_slot(p, side):
                return scratch[p, side].rearrange("h (d s) t -> (h d) s t", s=SLOTS)

            def load_tokens(it, off):
                p = it.slot(off)
                sp.wait_ge(xt_ps, floor0(it.unit(off - 1)))
                sp.dma_start(h_in[p][:, :, :], x[it.batch(off)].rearrange("(t p) c -> p t c", p=P)).then_inc(h_loaded[p], 16)

            def store_parts(it, off):
                p = it.slot(off)
                for side, slots in ((0, Q_SLOTS), (1, K_SLOTS)):
                    sp.wait_ge(part2[side], it.unit(off + 1))
                    for g in range(GROUPS):
                        sp.wait_ge(qk_loaded[p][g], floor0(it.same_parity_before(off) * 32))
                    sp.sem_inc(sp_stands, 1)
                    for part in range(PARTS):
                        place = by_slot(p, side)[:, slots[part], :]
                        sp.dma_start(place, parts[side][:, part, :].unsqueeze(1).to_broadcast(place.shape)).then_inc(stored[side], 16)

            def load_group(it, off, g):
                p = it.slot(off)
                for side in range(2):
                    sp.wait_ge(stored[side], it.unit(off + 1) * (16 * PARTS))
                sp.sem_inc(sp_stands, 1)
                if it.exists(off - 2):
                    types = len(CHUNKS[it.layer(off - 2)])
                    sp.wait_ge(scores_ready, chunks_before(it, off - 2) + (g + 1) * types * GROUP)
                    sp.sem_inc(sp_stands, 1)
                heads = slice(g * GROUP, (g + 1) * GROUP)
                for side, stack in ((0, q_st[p]), (1, k_st[p])):
                    sp.dma_start(stack[0:STACK_ROWS, heads, :], scratch[p, side, heads].rearrange("h r t -> r h t")).then_inc(qk_loaded[p][g], 16)

            def write_shift(it, off):
                p = it.slot(off)
                sp.wait_ge(lo_ready, it.unit(off + 1))
                for g in range(GROUPS):
                    sp.wait_ge(qk_loaded[p][g], (it.same_parity_before(off) + 1) * 32)
                for row, shift in zip(SHIFT_ROWS, (shift_hi, shift_lo)):
                    sp.dma_start(q_st[p][row:row + 1, :, :], shift[:, :]).then_inc(shift_in[p], 16)

            def iteration(it):
                if it.exists(2) and it.layer(2) == LOCAL and it.rep >= 0:
                    load_tokens(it, 2)
                if it.rep == 0:
                    sp.dma_start(tokens[:, :, :, :].rearrange("p b t c -> p (b t) c"),
                                 x.rearrange("b (t p) c -> p (b t) c", p=P)).then_inc(tokens_in, 16)
                    sp.dma_start(pack[:, :, PACK_B2:PACK], bias2.unsqueeze(0).to_broadcast([P, E, C])).then_inc(moe_w, 16)
                if it.exists(0) and it.layer(0) == LOCAL:
                    e = it.unit(0)
                    sp.dma_start(pack[:, e, PACK_W1:PACK_W2], w1[e]).then_inc(moe_w, 16)
                    sp.dma_start(pack[:, e, PACK_W2:PACK_B1].rearrange("p (f c) -> p f c", c=C),
                                 w2[e].rearrange("(f p) c -> p f c", p=P)).then_inc(moe_w, 16)
                    share = table.rearrange("(n p r) c -> n p r c", n=B, p=P)
                    sp.dma_start(share[it.unit(0)], spare_row.unsqueeze(1).to_broadcast([P, TABLE_ROWS // (B * P), ROW])
                                 ).then_inc(spared, 16)
                if it.exists(2):
                    store_parts(it, 2)
                if it.exists(1) and it.layer_now == CAUSAL:
                    write_shift(it, 1)
                if it.exists(2):
                    for g in range(GROUPS - 1):
                        load_group(it, 2, g)
                if it.exists(1) and it.layer_now == LOCAL:
                    write_shift(it, 1)
                if it.exists(2):
                    load_group(it, 2, GROUPS - 1)

            for first in range(2):
                load_tokens(Iteration(first // 2 - 1, first - 2), 2)
            sp.wait_ge(consts, 1)
            for p in range(2):
                for side, constant in ((0, zeros_b), (1, ones_b)):
                    sp.dma_start(by_slot(p, side)[:, SLOTS - 1, :], constant).then_inc(shift_rows, 16)
            sp.wait_ge(shift_rows, 64)
            sp.wait_ge(zeroed, 2)
            sp.wait_ge(pool_zeroed, 2)
            sp.wait_ge(consts, 4)
            run(sp, iteration)

            sp.wait_ge(setup_sb, 1)
            sp.wait_ge(moe_w, MOE_LOADS)
            sp.wait_ge(scores_ready, CHUNKS_ALL)
            sp.wait_ge(planned, 1)

            def load_weights(n, w):
                expert = nc.values_load(block_expert[0:1, bass.ds(n, 1)], engines=[mybir.EngineType.SP], min_val=0, max_val=E - 1)
                sp.dma_start(block_w[w], pack[:, bass.ds(expert, 1), :].rearrange("p e w -> p (e w)")).then_inc(w_in[w], 16)

            def stage(n, like, turn):
                if like >= BLOCKS:
                    return
                i, w = like % DEPTH, like % W_DEPTH
                if like >= DEPTH:
                    sp.wait_ge(y_out[i], turn * (BLT * 16))
                    sp.sem_inc(sp_stands, 1)
                first = nc.values_load(block_row[0:1, bass.ds(n, 1)], engines=[mybir.EngineType.SP], min_val=0,
                                       max_val=TABLE_ROWS - BLK)
                sp.dma_start(block_x[i], table[bass.ds(first, BLK), :].rearrange("(t p) c -> p t c", p=P)).then_inc(x_in[i], 16)
                if like >= W_DEPTH:
                    sp.wait_ge(block_done, n - (W_DEPTH - 1))
                    sp.sem_inc(sp_stands, 1)
                    load_weights(n, w)

            for n in range(W_DEPTH):
                load_weights(n, n)
            sp.wait_ge(rows_out, B * CHOICES * 16)
            run_blocks(sp, stage)
            for done in y_out:
                sp.wait_ge(done, BLOCKS // DEPTH * BLT * 16)

            by_choice = outputs.rearrange("(r n p) c -> r p n c", r=TOP, p=P)
            for share in range(SHARES):
                for r, place in enumerate((first_tiles, second_tiles)):
                    sp.dma_start(place[:, tiles(share), :], by_choice[r][:, tiles(share), :]).then_inc(y_in[share], 16)
            sp.wait_ge(result_out, 16 * SHARES)

        @block.gpsimd
        def _(pool):
            nc.gpsimd.memset(neg_half[:, :], -0.5)
            nc.gpsimd.memset(zeros_b, 0.0)
            nc.gpsimd.memset(ones_b, 1.0).then_inc(consts, 1)
            nc.gpsimd.memset(ident[:, :], 0.0)
            for mask in mask_b.values():
                last = nc.gpsimd.memset(mask[:, :], 0.0)
            last.then_inc(consts, 1)
            pool.wait_ge(consts, 2)
            nc.gpsimd.affine_select(out=ident[:, :], in_=ident[:, :], compare_op=ALU.not_equal, fill=1.0, base=0,
                                    pattern=[[-1, P]], channel_multiplier=1)
            nc.gpsimd.affine_select(out=mask_b[LOCAL][:, 0:P], in_=mask_b[LOCAL][:, 0:P], compare_op=ALU.is_ge, fill=NEG, base=0,
                                    pattern=[[1, P]], channel_multiplier=-1)
            for mask, keys in ((mask_b[LOCAL], 2 * P), (mask_b[CAUSAL], T)):
                nc.gpsimd.affine_select(out=mask[:, keys - P:keys], in_=mask[:, keys - P:keys], compare_op=ALU.is_ge, fill=NEG, base=0,
                                        pattern=[[-1, P]], channel_multiplier=1)
            nc.gpsimd.iota(expert_ids[:, :, :], pattern=[[0, NT], [1, E]], base=0, channel_multiplier=0,
                           allow_small_or_imprecise_dtypes=True).then_inc(consts, 1)
            nc.gpsimd.memset(spare_row[:, 0:PLACE], 0.0)
            nc.gpsimd.iota(spare_row[:, PLACE:ROW].bitcast(U32), pattern=[[0, 1]], base=TOP * N, channel_multiplier=0).then_inc(consts, 1)
            for stack in k_st:
                nc.gpsimd.memset(words(stack), 0.0).then_inc(pool_zeroed, 1)
            nc.gpsimd.memset(onehot[:, :, :], 0.0)
            nc.gpsimd.memset(square_b[:, :], 1.0)
            nc.gpsimd.memset(tri_b[:, :], 1.0).then_inc(consts, 1)
            nc.gpsimd.iota(next_row[:, :], pattern=[[SEG, E]], base=0, channel_multiplier=0, allow_small_or_imprecise_dtypes=True)
            nc.gpsimd.iota(places[:, :, :, :], pattern=[[T, B], [N, TOP], [P, NT]], base=0, channel_multiplier=1)
            pool.wait_ge(consts, 5)
            nc.gpsimd.affine_select(out=tri_b[:, :], in_=tri_b[:, :], compare_op=ALU.is_ge, fill=0.0, base=-1,
                                    pattern=[[1, P]], channel_multiplier=-1).then_inc(consts, 1)

            def plan_constants():
                pool.wait_ge(stored[0], UNITS * (16 * PARTS))
                nc.gpsimd.memset(not_after, 1.0).then_inc(plan_consts, 1)
                nc.gpsimd.iota(block_from, pattern=[[SEG, E], [BLK, SEG_BLOCKS]], base=0, channel_multiplier=0,
                               allow_small_or_imprecise_dtypes=True)
                nc.gpsimd.iota(block_no, pattern=[[1, BLOCKS]], base=0, channel_multiplier=0, allow_small_or_imprecise_dtypes=True)
                pool.wait_ge(plan_consts, 1)
                nc.gpsimd.affine_select(out=not_after, in_=not_after, compare_op=ALU.is_ge, fill=0.0, base=0,
                                        pattern=[[1, E], [-1, E]], channel_multiplier=0).then_inc(plan_consts, 1)

            def send(b, j):
                if j == 0:
                    pool.wait_ge(placing, (b + 1) * len(PLACING))
                    pool.wait_ge(rows_copied, b + 1)
                    pool.wait_ge(rows_ready, b + 1)
                    pool.wait_ge(spared, B * 16)
                    pool.sem_inc(pool_stands, 1)
                nc.gpsimd.indirect_dma_start(out=table[:, :], out_offset=bass.IndirectOffsetOnAxis(ap=row_at[:, j:j + 1], axis=0),
                                             in_=rows[:, j // NT, j % NT, :], in_offset=None, bounds_check=TABLE_ROWS - 1,
                                             oob_is_err=False).then_inc(rows_out, 16)

            def root(kind, n):
                pool.wait_ge(LN[kind][2], n + 1)
                _, _, var_eps, rstd = norm_sb[kind]
                nc.gpsimd.tensor_tensor(rstd[:, :], var_eps[:, :], neg_half[:, :], ALU.pow).then_inc(LN[kind][3], 1)

            def iteration(it):
                types = len(CHUNKS[it.layer_now])
                for k in range(it.steps):
                    def roots():
                        if "h_root" in it.norms(k) and it.exists(2) and it.layer(2) == CAUSAL:
                            root("h", it.batch(2))
                        if "root" in it.norms(k) and it.exists(-1):
                            root("x1" if it.layer(-1) == LOCAL else "moe", it.batch(-1))

                    if not it.exists(0):
                        roots()
                    if it.exists(0):
                        chunk = CHUNKS[it.layer_now][k % types]
                        own = [col for _, _, _, col in chunk]
                        ahead = [col + P for _, _, n, col in chunk if it.layer_now == LOCAL and n > P]
                        for c in range(GROUP):
                            n = k * GROUP + c
                            if c == 2 and it.layer_now == LOCAL:
                                roots()
                            pool.wait_ge(exp_done, chunks_before(it, 0) + n + 1)
                            pool.sem_inc(pool_stands, 1)
                            for columns, sign in ((own, 1), (ahead, -1)):
                                if not columns:
                                    continue
                                step = columns[-1] - columns[0] or P
                                view = probs[:, n % RING, columns[0]:columns[-1] + P]
                                if len(columns) > 1:
                                    view = probs[:, n % RING, :].rearrange("p (n q) -> p n q", q=P)[
                                        :, columns[0] // P:columns[-1] // P + 1:step // P, :]
                                    pattern = [[0, len(columns)], [sign, P]]
                                else:
                                    pattern = [[sign, P]]
                                last = nc.gpsimd.affine_select(out=view, in_=view, compare_op=ALU.is_ge, fill=0.0, base=0,
                                                               pattern=pattern, channel_multiplier=-sign)
                            last.then_inc(masked, 1)
                    if it.layer_now == CAUSAL and it.exists(0):
                        roots()
                    if "root" in it.norms(k) and it.exists(-1) and it.layer(-1) == CAUSAL:
                        b = it.batch(-1)
                        pool.wait_ge(h_ready, b + 1)
                        pool.sem_inc(pool_stands, 1)
                        nc.gpsimd.tensor_tensor(resid[:, b, :, :], y[:, :, :], resid[:, b, :, :], ALU.add).then_inc(sum_ready, 1)
                    if "qk" in it.taken(k - 1) and it.exists(2):
                        for side in range(2):
                            pool.wait_ge(part1[side], it.unit(3))
                            nc.gpsimd.tensor_tensor(parts[side][:, 2, :], rest[side][:, :], parts[side][:, 1, :],
                                                    ALU.subtract).then_inc(part2[side], 1)
                    if it.exists(-2) and it.layer(-2) == CAUSAL and k in SEND_STEPS:
                        for r in range(TOP):
                            send(it.batch(-2), (k - SEND_STEPS[0]) * TOP + r)

            run(pool, iteration)
            plan_constants()
            for j in range(CHOICES):
                send(B - 1, j)

            def stage(m, like, turn):
                if like < 2:
                    return
                n, i = m - 2, like % 2
                pool.wait_ge(block_done, n + 1)
                pool.sem_inc(pool_stands, 1)
                for t in range(BLT):
                    place = block_x[(like - 2) % DEPTH][:, t, PLACE:ROW].bitcast(U32)
                    nc.gpsimd.indirect_dma_start(out=outputs[:, :], out_offset=bass.IndirectOffsetOnAxis(ap=place, axis=0),
                                                 in_=block_y[i][:, t, :], in_offset=None, bounds_check=TOP * N - 1,
                                                 oob_is_err=False).then_inc(y_out[(like - 2) % DEPTH], 16)

            run_blocks(pool, stage)

            pool.wait_ge(pv_done, STEPS_ALL)
            nc.gpsimd.memset(halves, -0.5).then_inc(halves_ready, 1)
            pool.wait_ge(halves_ready, 1)

            def both(share):
                pool.wait_ge(y_in[share], 32)
                nc.gpsimd.tensor_tensor(first_tiles[:, tiles(share), :], first_tiles[:, tiles(share), :], second_tiles[:, tiles(share), :],
                                        ALU.add).then_inc(pair_sum, 1)

            both(0)
            for share in range(SHARES):
                if share + 1 < SHARES:
                    both(share + 1)
                pool.wait_ge(final_done, share * len(FINAL) + 3)
                nc.gpsimd.tensor_tensor(final_rstd[:, tiles(share), :], final_var[:, tiles(share), :], halves[:, tiles(share), :],
                                        ALU.pow).then_inc(final_root, 1)

        @block.scalar
        def _(act):
            act.dma_start(wq1_raw, w_qkv1.rearrange("(s o) c -> o s c", o=P)).then_inc(raw_w, 16)
            act.dma_start(wo1_raw, w_out1).then_inc(raw_w, 16)
            act.dma_start(bias1_raw, bias1.rearrange("e (f p) -> (e f) p", p=P)).then_inc(raw_w, 16)
            act.dma_start(wq_sb[1][:, :], w_qkv2).then_inc(attn_w, 16)
            act.dma_start(wo_sb[1][:, :], w_o2).then_inc(attn_w, 16)
            act.dma_start(wg_sb[:, :], w_gate).then_inc(attn_w, 16)
            for i, v in enumerate((g1, b1, g2, b2)):
                act.dma_start(norms[:, i:i + 1], v.unsqueeze(1)).then_inc(attn_w, 16)
            act.wait_ge(setup_ps, 2)
            nc.scalar.activation(wq_sb[0][:, :], misc[0][:, 0:3 * C], ACT.Copy)
            nc.scalar.activation(wo_sb[0][:, :], misc[1][:, 0:C], ACT.Copy)
            nc.scalar.activation(pack[:, :, PACK_B1:PACK_B2], misc[1][:, C:C + E * FT].rearrange("p (e f) -> p e f", f=FT),
                                 ACT.Copy).then_inc(setup_sb, 1)

            def copy_o(it, off, g):
                types = len(CHUNKS[it.layer(off)])
                act.wait_ge(pv_done, steps_before(it, off) + (g + 1) * types)
                act.wait_ge(ot_ps, floor0(it.unit(off - 1) * NT))
                nc.scalar.activation(o_t[it.slot(off)][:, g, :], o_ps[:, :], ACT.Copy).then_inc(o_copied, 1)

            def copies(it, k):
                types = len(CHUNKS[it.layer_now])
                if k == 1 and it.exists(-1):
                    copy_o(it, -1, GROUPS - 1)
                if k > types and k % types == 1 and it.exists(0):
                    copy_o(it, 0, k // types - 1)

            def take(it, k):
                if "on" in it.taken(k) and it.exists(-1):
                    act.wait_ge(ont_ps, it.unit(0))
                    act.wait_ge(proj_ps, floor0(it.unit(-1)))
                    if it.exists(-2) and it.layer(-2) == CAUSAL:
                        act.wait_ge(logits_ps, it.batch(-1))
                    nc.scalar.activation(o_norm_t[:, :], misc[0][:, :], ACT.Copy).then_inc(ont_sb, 1)
                if "xt" in it.taken(k) and it.exists(2):
                    act.wait_ge(xt_ps, it.unit(3))
                    act.wait_ge(v_ps, floor0(it.unit(2)))
                    if it.layer(2) == LOCAL:
                        nc.scalar.activation(x_t[:, :], misc[0][:, :], ACT.Copy).then_inc(xt_sb, 1)
                    else:
                        nc.scalar.activation(x_t[:, :], misc[0][:, :], ACT.Identity, scale=norms[:, 0:1],
                                             bias=norms[:, 1:2]).then_inc(xt_sb, 1)
                if "qk" in it.taken(k) and it.exists(2):
                    for side, filled, ps in ((0, q_ps, misc[1]), (1, k_ps, misc[0])):
                        act.wait_ge(filled, it.unit(3))
                        act.wait_ge(stored[side], floor0(it.unit(2) * (16 * PARTS)))
                        nc.scalar.activation(parts[side][:, 0, :], ps[:, :], ACT.Copy).then_inc(part0[side], 1)
                if "qk" in it.taken(k - 1) and it.exists(2):
                    for side in range(2):
                        act.wait_ge(rest_ready[side], it.unit(3))
                        nc.scalar.activation(parts[side][:, 1, :], rest[side][:, :], ACT.Copy).then_inc(part1[side], 1)
                if it.exists(-1) and it.layer(-1) == CAUSAL:
                    if "xf" in it.taken(k):
                        act.wait_ge(xf_ps, it.batch(0))
                        act.wait_ge(proj_ps, it.unit(0))
                        nc.scalar.activation(moe_in_t[:, :], misc[1][:, :], ACT.Identity, scale=norms[:, 2:3],
                                             bias=norms[:, 3:4]).then_inc(xf_sb, 1)
                    if "xf" in it.taken(k - 1):
                        act.wait_ge(moe_in_ready, it.batch(0))
                        act.wait_ge(rows_out, floor0(it.batch(-1) * (CHOICES * 16)))
                        nc.scalar.activation(rows[:, 1, :, 0:C], rows[:, 0, :, 0:C], ACT.Copy).then_inc(rows_copied, 1)
                    if "route" in it.taken(k - 1):
                        act.wait_ge(routed, it.batch(-1) * len(ROUTE) + 2)
                        nc.scalar.activation(gap_exp[:, :], gap[:, :], ACT.Exp).then_inc(gap_exped, 1)

            def iteration(it):
                types = len(CHUNKS[it.layer_now])
                for k in range(it.steps):
                    if not it.exists(0):
                        copies(it, k)
                        take(it, k)
                    if it.exists(0):
                        width = sum(n for _, _, n, _ in CHUNKS[it.layer_now][k % types])
                        for c in range(GROUP):
                            n = k * GROUP + c
                            if c == 1:
                                copies(it, k)
                            if c == 2:
                                take(it, k)
                            act.wait_ge(scores_ready, chunks_before(it, 0) + n + 1)
                            act.wait_ge(pv_done, floor0(steps_before(it, 0) + (k - 1)))
                            nc.scalar.activation(probs[:, n % RING, 0:width], score_ps[n % 2][:, 0:width], ACT.Exp,
                                                 scale=SCALE).then_inc(exp_done, 1)

            run(act, iteration)
            act.wait_ge(pv_done, STEPS_ALL)
            act.wait_ge(v_ps, UNITS)

            def stage(m, like, turn):
                if 1 <= like <= BLOCKS:
                    n, i, w = m - 1, (like - 1) % 2, (like - 1) % W_DEPTH
                    if like >= 3:
                        act.wait_ge(block_ps, n - 1)
                    for f in range(FT):
                        if f % 2 == 0:
                            act.wait_ge(hidden_filled, n * PAIRS + (f // 2 + 1))
                        nc.scalar.activation(hidden[:, i * FT + f, 0:BLK], hidden_ps[2 * i + f // 2][:, f % 2 * BLK:(f % 2 + 1) * BLK],
                                             ACT.Gelu_apprx_tanh, bias=block_w[w][:, PACK_B1 + f:PACK_B1 + f + 1]).then_inc(hidden_ready, 1)
                if like < BLOCKS:
                    act.wait_ge(bx_ps, m + 1)
                    if like >= 2:
                        act.wait_ge(hidden_filled, (m - 1) * PAIRS)
                    nc.scalar.activation(block_xt[like % 2], misc[like % 2][:, 0:BLK], ACT.Identity, scale=norms[:, 2:3],
                                         bias=norms[:, 3:4]).then_inc(bx_sb, 1)

            run_blocks(act, stage)

            def apply(share):
                act.wait_ge(final_root, share + 1)
                act.wait_ge(centred, share + 1)
                for t in range(B * NT)[tiles(share)]:
                    last = nc.scalar.activation(first_tiles[:, t, :], sum_tiles[:, t, :], ACT.Identity, scale=final_rstd[:, t, :])
                last.then_inc(result_ready, 1)
                act.wait_ge(result_ready, share + 1)
                rows_of = out.rearrange("b (t p) c -> p (b t) c", p=P)
                act.dma_start(rows_of[:, tiles(share), :], first_tiles[:, tiles(share), :]).then_inc(result_out, 16)

            for share in range(SHARES):
                act.wait_ge(final_done, (share + 1) * len(FINAL))
                for t in range(B * NT)[tiles(share)]:
                    last = nc.scalar.activation(sum_tiles[:, t, :], sum_tiles[:, t, :], ACT.Identity, bias=final_negmean[:, t, :])
                last.then_inc(centred, 1)
                apply(share)

        @block.vector
        def _(dve):
            for stack in q_st:
                nc.vector.memset(stack[:, :, :].rearrange("p h t -> p (h t)").bitcast(F32), 0.0).then_inc(zeroed, 1)
            for i, va in enumerate(v_aug):
                nc.vector.memset(va[:, :, :, :], 0.0).then_inc(va_cleared, 1)
            for i, va in enumerate(v_aug):
                dve.wait_ge(va_cleared, i + 1)
                nc.vector.memset(va[:, :, :, HD:HD + 1], 1.0).then_inc(zeroed, 1)

            def norm_stats(kind, n, source, ready):
                stats_done, mean_done, var_done, _ = LN[kind]
                stats, mean_var, var_eps, _ = norm_sb[kind]
                dve.wait_ge(ready, n)
                for t in range(NT):
                    last = nc.vector.bn_stats(stats[:, t, :], source[:, t, :])
                last.then_inc(stats_done, 1)
                dve.wait_ge(stats_done, n + 1)
                dve.sem_inc(dve_stands, 1)
                for t in range(NT):
                    last = nc.vector.bn_aggr(mean_var[:, t, :], stats[:, t, :])
                last.then_inc(mean_done, 1)
                dve.wait_ge(mean_done, n + 1)
                nc.vector.tensor_scalar(var_eps[:, :], mean_var[:, :, 1], EPS, None, ALU.add).then_inc(var_done, 1)

            def norm_apply(kind, n, source, target, ready):
                _, mean_var, _, rstd = norm_sb[kind]
                dve.wait_ge(LN[kind][3], n + 1)
                for t in range(NT):
                    last = nc.vector.tensor_scalar(target[:, t, :], source[:, t, :], mean_var[:, t, 0:1], rstd[:, t:t + 1],
                                                   ALU.subtract, ALU.mult)
                last.then_inc(ready, 1)

            def divide(it, t):
                n = it.unit(-1) * NT + t
                o_view = misc[t % 2][:, :].rearrange("p (h w) -> p h w", w=QUAD)
                dve.wait_ge(on_ready, n)
                dve.wait_ge(ot_ps, n + 1)
                nc.vector.reciprocal(inv_sum[:, :].unsqueeze(2), o_view[:, :, HD:HD + 1]).then_inc(inv_ready, 1)
                dve.wait_ge(inv_ready, n + 1)
                dve.wait_ge(ont_ps, floor0(it.unit(-1)))
                if it.exists(-2):
                    if it.layer(-2) == LOCAL:
                        dve.wait_ge(x1_ready, it.batch(-1) if it.layer(-1) == LOCAL else B)
                    else:
                        dve.wait_ge(moe_in_ready, it.batch(-1))
                        dve.wait_ge(sum_ready, it.batch(-1))
                nc.vector.tensor_tensor(o_norm[:, t, :].rearrange("p (h d) -> p h d", d=HD), o_view[:, :, 0:HD],
                                        inv_sum[:, :].unsqueeze(2).to_broadcast([P, H, HD]), ALU.mult).then_inc(on_ready, 1)

            def finish(it):
                dve.wait_ge(proj_ps, it.unit(0))
                b = it.batch(-1)
                proj = misc[1][:, :].rearrange("p (t c) -> p t c", c=C)
                if it.layer(-1) == LOCAL:
                    dve.wait_ge(tokens_in, 16)
                    dve.wait_ge(x1_ready, b)
                    nc.vector.tensor_tensor(y[:, :, :], proj, tokens[:, b, :, :], ALU.add).then_inc(y_ready, 1)
                else:
                    dve.wait_ge(x1_ready, B)
                    dve.wait_ge(moe_in_ready, b)
                    dve.wait_ge(sum_ready, b)
                    nc.vector.tensor_tensor(y[:, :, :], proj, resid[:, b, :, :], ALU.add).then_inc(y_ready, 1)

            def finish_stats(it):
                dve.wait_ge(y_ready, it.unit(0))
                if it.layer(-1) == LOCAL:
                    norm_stats("x1", it.batch(-1), y, x1_ready)
                else:
                    norm_stats("moe", it.batch(-1), y, moe_in_ready)

            def finish_norm(it):
                b = it.batch(-1)
                if it.layer(-1) == LOCAL:
                    norm_apply("x1", b, y, resid[:, b, :, :], x1_ready)
                else:
                    dve.wait_ge(xf_ps, floor0(b))
                    dve.wait_ge(rows_out, floor0(b * (CHOICES * 16)))
                    dve.wait_ge(spared, B * 16)
                    norm_apply("moe", b, y, rows[:, 0, :, 0:C], moe_in_ready)

            def route(it):
                b = it.batch(-1)
                done = {name: b * len(ROUTE) + (i + 1) for i, name in enumerate(ROUTE)}
                dve.wait_ge(routed, b * len(ROUTE))
                dve.wait_ge(logits_ps, b + 1)
                nc.vector.tensor_copy(logits[:, :, :].rearrange("p t e -> p (t e)"), misc[1][:, 0:NT * E]).then_inc(logits_sb, 1)
                dve.wait_ge(logits_sb, b + 1)
                dve.sem_inc(dve_stands, 1)
                for t in range(NT):
                    last = nc.vector.max(top_val[:, t, :], logits[:, t, :])
                last.then_inc(routed, 1)
                dve.wait_ge(routed, done["vals"])
                dve.sem_inc(dve_stands, 1)
                for t in range(NT):
                    nc.vector.max_index(top_idx[:, t, :], top_val[:, t, :], logits[:, t, :])
                nc.vector.tensor_tensor(gap[:, :], top_val[:, :, 1], top_val[:, :, 0], ALU.subtract).then_inc(routed, 1)
                dve.wait_ge(routed, done["idx"])
                nc.vector.tensor_copy(top_idf[:, :, :], top_idx[:, :, 0:TOP]).then_inc(routed, 1)

                dve.wait_ge(routed, done["idf"])
                dve.wait_ge(consts, 6)
                dve.wait_ge(ranked, b)
                dve.wait_ge(placing, b * len(PLACING))
                for r in range(TOP):
                    nc.vector.tensor_tensor(chosen[:, r * NT:(r + 1) * NT, :], expert_ids[:, :, :],
                                            top_idf[:, :, r:r + 1].to_broadcast([P, NT, E]), ALU.is_equal).then_inc(routed, 1)

            def place(it):
                b = it.batch(-1)
                done = {name: b * len(PLACING) + (i + 1) for i, name in enumerate(PLACING)}
                earlier = misc[1][:, 0:(CHOICES + 1) * E].rearrange("p (n e) -> p n e", e=E)
                dve.wait_ge(ranked, b + 1)
                dve.wait_ge(placing, b * len(PLACING))
                nc.vector.tensor_tensor(row_of[:, :, :], earlier[:, 0:CHOICES, :], next_row[:, :].unsqueeze(1).to_broadcast([P, CHOICES, E]),
                                        ALU.add).then_inc(placing, 1)
                dve.wait_ge(placing, done["at"])
                nc.vector.tensor_tensor(next_row[:, :], next_row[:, :], earlier[:, CHOICES, :], ALU.add).then_inc(placing, 1)
                nc.vector.tensor_tensor(row_of[:, :, :], row_of[:, :, :], chosen, ALU.mult).then_inc(placing, 1)
                dve.wait_ge(placing, done["own"])
                nc.vector.tensor_reduce(row_f[:, :], row_of[:, :, :], AX_X, ALU.add).then_inc(placing, 1)
                dve.wait_ge(placing, done["sum"])
                dve.wait_ge(rows_out, b * (CHOICES * 16))
                nc.vector.tensor_copy(row_at[:, :], row_f[:, :]).then_inc(placing, 1)

            def weigh(it):
                b = it.batch(-1)
                done = {name: b * len(ROUTE) + (i + 1) for i, name in enumerate(ROUTE)}
                weight = [rows[:, r, :, WEIGHT:WEIGHT + 1].rearrange("p t c -> p (t c)") for r in range(TOP)]
                dve.wait_ge(gap_exped, b + 1)
                nc.vector.tensor_scalar(gap_sum[:, :], gap_exp[:, :], 1.0, None, ALU.add).then_inc(routed, 1)
                dve.wait_ge(routed, done["sum"])
                nc.vector.reciprocal(weight[0], gap_sum[:, :]).then_inc(routed, 1)
                for r in range(TOP):
                    nc.vector.tensor_copy(rows[:, r, :, PLACE:ROW].bitcast(U32).rearrange("p t c -> p (t c)"), places[:, b, r, :])
                dve.wait_ge(routed, done["w0"])
                nc.vector.tensor_tensor(weight[1], gap_exp[:, :], weight[0], ALU.mult).then_inc(rows_ready, 1)

            def norm_input(it, k):
                if it.exists(2) and it.layer(2) == CAUSAL:
                    b = it.batch(2)
                    if "h_stats" in it.norms(k):
                        dve.wait_ge(x1_ready, b + 1)
                        norm_stats("h", b, resid[:, b, :, :], h_ready)
                    if "h_norm" in it.norms(k):
                        dve.wait_ge(xt_ps, it.unit(1))
                        norm_apply("h", b, resid[:, b, :, :], h_in[it.slot(2)], h_ready)

            def maxima(it, banks):
                for n in banks:
                    i, h, heads, _, keys = BANKS[it.layer(1)][n]
                    p = it.slot(1)
                    dve.wait_ge(max_filled, banks_before(it, 1) + (n + 1))
                    dve.wait_ge(maxt_ps, floor0(it.unit(0)))
                    dve.sem_inc(dve_stands, 1)
                    for m in range(heads):
                        scores = max_ps[n % MAX_BANKS][:, m * keys:(m + 1) * keys]
                        masks = mask_b[it.layer(1)]
                        last = nc.vector.tensor_tensor_reduce(out=scores, in0=scores, in1=masks[:, masks.shape[1] - keys:], scale=1.0,
                                                              scalar=NEG, op0=ALU.add, op1=ALU.max,
                                                              accum_out=row_max[p][:, i, h + m:h + m + 1])
                    last.then_inc(max_taken, 1)

            def take_v(it):
                dve.wait_ge(v_ps, it.unit(2))
                dve.wait_ge(zeroed, 4)
                dve.wait_ge(pv_done, floor0(steps_before(it, 0)))
                nc.vector.tensor_copy(v_aug[it.slot(1)][:, :, :, 0:HD].rearrange("p t h d -> p (t h) d"),
                                      misc[1][:, :].rearrange("p (n d) -> p n d", d=HD)).then_inc(v_ready, 1)

            def take(it, k):
                if it.exists(-1) and it.layer(-1) == CAUSAL:
                    if "route" in it.taken(k):
                        route(it)
                    if "rank" in it.taken(k):
                        place(it)
                    if "weigh" in it.norms(k):
                        weigh(it)
                if "shift" in it.taken(k) and it.exists(1):
                    p = it.slot(0)
                    dve.wait_ge(maxt_ps, it.unit(2))
                    if it.exists(0):
                        dve.wait_ge(shift_in[p], (it.same_parity_before(0) + 1) * 32)
                    nc.vector.tensor_scalar(shift_hi[:, :], misc[0][0:H, :], -1.0, None, ALU.mult).then_inc(hi_ready, 1)
                    dve.wait_ge(hi_ready, it.unit(2))
                    nc.vector.scalar_tensor_tensor(out=shift_lo[:, :], in0=misc[0][0:H, :], scalar=-1.0, in1=shift_hi[:, :],
                                                   op0=ALU.mult, op1=ALU.subtract).then_inc(lo_ready, 1)
                if it.exists(-1) and "out" in it.taken(k):
                    finish(it)

            def split_rest(it, side):
                dve.wait_ge(part0[side], it.unit(3))
                dve.wait_ge(part2[side], floor0(it.unit(2)))
                nc.vector.tensor_tensor(rest[side][:, :], misc[1 - side][:, :], parts[side][:, 0, :],
                                        ALU.subtract).then_inc(rest_ready[side], 1)

            def take_late(it, k):
                if it.exists(-1) and "stats" in it.norms(k):
                    finish_stats(it)
                if "norm" in it.norms(k) and it.exists(-1):
                    finish_norm(it)

            def iteration(it):
                for k in range(it.steps):
                    banks = it.banks_at(k)
                    half = len(banks) // 2
                    divided = [t for t in range(NT) if f"t{t}" in it.taken(k) and it.exists(-1)]
                    if it.layer_now == LOCAL:
                        norm_input(it, k)
                        take(it, k)
                        for t in divided:
                            divide(it, t)
                        maxima(it, banks[:half])
                        if "qk" in it.taken(k) and it.exists(2):
                            for side in range(2):
                                split_rest(it, side)
                        maxima(it, banks[half:])
                        if "v" in it.taken(k) and it.exists(1):
                            take_v(it)
                        take_late(it, k)
                    else:
                        if "v" in it.taken(k) and it.exists(1):
                            take_v(it)
                        take(it, k)
                        for piece in range(2):
                            for t in divided[piece:piece + 1]:
                                divide(it, t)
                            if "qk" in it.taken(k - 1) and it.exists(2):
                                split_rest(it, piece)
                            maxima(it, banks[:half][piece:piece + 1])
                        norm_input(it, k)
                        take_late(it, k)
                        maxima(it, banks[half:])

            run(dve, iteration)

            def plan():
                PLAN = ("used", "blocks", "end_terms", "end", "skip", "past", "expert", "limited", "past_rows", "rows", "first")
                done = {name: i + 1 for i, name in enumerate(PLAN)}
                blocks = [P, BLOCKS, E]
                dve.wait_ge(placing, B * len(PLACING))
                dve.wait_ge(plan_consts, 2)
                for side in range(2):
                    dve.wait_ge(part2[side], UNITS)
                nc.vector.tensor_tensor(block_used, next_row[:, :].unsqueeze(2).to_broadcast([P, E, SEG_BLOCKS]),
                                        block_from, ALU.is_gt).then_inc(planning, 1)
                dve.wait_ge(planning, done["used"])
                nc.vector.tensor_reduce(blocks_of[:, :], block_used, AX_X, ALU.add).then_inc(planning, 1)
                dve.wait_ge(planning, done["blocks"])
                nc.vector.tensor_tensor(end_terms, blocks_of[:, :].unsqueeze(1).to_broadcast([P, E, E]), not_after,
                                        ALU.mult).then_inc(planning, 1)
                dve.wait_ge(planning, done["end_terms"])
                nc.vector.tensor_reduce(end_block[:, :], end_terms, AX_X, ALU.add).then_inc(planning, 1)
                nc.vector.tensor_scalar(skip_rows[:, :], blocks_of[:, :], -float(BLK), float(SEG), ALU.mult, ALU.add).then_inc(planning, 1)
                dve.wait_ge(planning, done["skip"])
                nc.vector.tensor_tensor(past, block_no.unsqueeze(2).to_broadcast(blocks),
                                        end_block[:, :].unsqueeze(1).to_broadcast(blocks), ALU.is_ge).then_inc(planning, 1)
                dve.wait_ge(planning, done["past"])
                nc.vector.tensor_reduce(block_f[:, 0, :], past, AX_X, ALU.add).then_inc(planning, 1)
                dve.wait_ge(planning, done["expert"])
                nc.vector.tensor_scalar(block_expert, block_f[:, 0, :], float(E - 1), None, ALU.min).then_inc(planning, 1)
                nc.vector.tensor_tensor(past, past, skip_rows[:, :].unsqueeze(1).to_broadcast(blocks),
                                        ALU.mult).then_inc(planning, 1)
                dve.wait_ge(planning, done["past_rows"])
                nc.vector.tensor_reduce(block_f[:, 1, :], past, AX_X, ALU.add).then_inc(planning, 1)
                dve.wait_ge(planning, done["rows"])
                nc.vector.scalar_tensor_tensor(out=block_row, in0=block_no, scalar=float(BLK), in1=block_f[:, 1, :],
                                               op0=ALU.mult, op1=ALU.add).then_inc(planned, 1)

            plan()
            dve.wait_ge(sum_ready, B)

            def stage(m, like, turn):
                if like < 2:
                    return
                n, i, d, w = m - 2, like % 2, (like - 2) % DEPTH, (like - 2) % W_DEPTH
                dve.wait_ge(block_ps, n + 1)
                if like >= 4:
                    dve.wait_ge(y_out[(like - 4) % DEPTH], loads(turn, like, 4) * (BLT * 16))
                nc.vector.tensor_tensor(block_y[i], y_ps[i][:, 0:BLK].rearrange("p (t c) -> p t c", c=C),
                                        block_w[w][:, PACK_B2:PACK].unsqueeze(1).to_broadcast([P, BLT, C]), ALU.add).then_inc(biased, 1)
                dve.wait_ge(biased, n + 1)
                for t in range(BLT):
                    last = nc.vector.tensor_scalar(block_y[i][:, t, :], block_y[i][:, t, :], block_x[d][:, t, WEIGHT:WEIGHT + 1], None,
                                                   ALU.mult)
                last.then_inc(block_done, 1)

            run_blocks(dve, stage)

            dve.wait_ge(halves_ready, 1)
            for share in range(SHARES):
                done = {name: share * len(FINAL) + (i + 1) for i, name in enumerate(FINAL)}
                dve.wait_ge(pair_sum, share + 1)
                nc.vector.tensor_tensor(sum_tiles[:, tiles(share), :], sum_tiles[:, tiles(share), :], first_tiles[:, tiles(share), :],
                                        ALU.add).then_inc(final_sum, 1)
                dve.wait_ge(final_sum, share + 1)
                for t in range(B * NT)[tiles(share)]:
                    last = nc.vector.bn_stats(final_stats[:, t, :], sum_tiles[:, t, :])
                last.then_inc(final_done, 1)
                dve.wait_ge(final_done, done["stats"])
                for t in range(B * NT)[tiles(share)]:
                    last = nc.vector.bn_aggr(final_mean[:, t, :], final_stats[:, t, :])
                last.then_inc(final_done, 1)
                dve.wait_ge(final_done, done["mean"])
                nc.vector.tensor_scalar(final_var[:, tiles(share), :], final_mean[:, tiles(share), 1:2], EPS, None, ALU.add).then_inc(final_done, 1)
                nc.vector.tensor_scalar(final_negmean[:, tiles(share), :], final_mean[:, tiles(share), 0:1], -1.0, None,
                                        ALU.mult).then_inc(final_done, 1)

        @block.tensor
        def _(pe):
            pe.wait_ge(consts, 3)
            pe.wait_ge(raw_w, RAW_LOADS)
            for s in range(3):
                last = nc.tensor.transpose(misc[0][:, s * C:(s + 1) * C], wq1_raw[:, s, :], ident[:, :])
            last.then_inc(setup_ps, 1)
            nc.tensor.transpose(misc[1][:, 0:C], wo1_raw, ident[:, :])
            nc.tensor.transpose(misc[1][:, C:C + E * FT], bias1_raw, ident[0:E * FT, 0:E * FT]).then_inc(setup_ps, 1)
            pe.wait_ge(zeroed, 2)
            nc.tensor.matmul(o_ps[:, :], q_st[0][:, 0, 0:P], q_st[0][:, 0, :], start=True, stop=True).then_inc(o_cleared, 1)
            pe.wait_ge(setup_sb, 1)
            pe.wait_ge(attn_w, ATTN_LOADS)

            def score_chunk(it, k, c):
                n = k * GROUP + c
                types = len(CHUNKS[it.layer_now])
                h = (k // types) * GROUP + c
                p = it.slot(0)
                if n == 0:
                    pe.wait_ge(shift_in[p], (it.same_parity_before(0) + 1) * 32)
                pe.wait_ge(exp_done, floor0(chunks_before(it, 0) + (n - 1)))
                for j, q0, width, col in CHUNKS[it.layer_now][k % types]:
                    last = nc.tensor.matmul(score_ps[n % 2][:, col:col + width], k_st[p][:, h, j * P:(j + 1) * P],
                                            q_st[p][:, h, q0:q0 + width], start=True, stop=True)
                last.then_inc(scores_ready, 1)

            def times_v(it, off, k):
                layer = it.layer(off)
                types = len(CHUNKS[layer])
                g, p = k // types, it.slot(off)
                pe.wait_ge(masked, chunks_before(it, off) + (k + 1) * GROUP)
                if k == 0:
                    pe.wait_ge(v_ready, it.unit(off + 1))
                if k % types == 0:
                    pe.wait_ge(o_copied, floor0(it.unit(off) * GROUPS + g))
                for j, q0, width, col in CHUNKS[layer][k % types]:
                    for c in range(GROUP):
                        slot = (k * GROUP + c) % RING
                        last = nc.tensor.matmul(o_ps[c * QUAD:c * QUAD + VW, q0:q0 + width], v_aug[p][:, j, g * GROUP + c, :],
                                                probs[:, slot, col:col + width], start=(j == 0), stop=(j == NT - 1),
                                                skip_group_check=True)
                last.then_inc(pv_done, 1)

            def max_bank(it, n):
                layer = it.layer(1)
                i, h0, heads, first, keys = BANKS[layer][n]
                p = it.slot(1)
                if i == 0 and first == 0 and h0 % GROUP == 0:
                    pe.wait_ge(qk_loaded[p][h0 // GROUP], (it.same_parity_before(1) + 1) * 32)
                pe.wait_ge(max_taken, floor0(banks_before(it, 1) + max(0, n - (MAX_BANKS - 1))))
                for m in range(heads):
                    last = nc.tensor.matmul(max_ps[n % MAX_BANKS][:, m * keys:(m + 1) * keys], q_st[p][:, h0 + m, i * P:(i + 1) * P],
                                            k_st[p][:, h0 + m, first:first + keys], start=True, stop=True)
                last.then_inc(max_filled, 1)

            def side_jobs(it, k):
                jobs = it.jobs(k)
                if "v" in jobs and it.exists(1):
                    pe.wait_ge(rest_ready[0], it.unit(2))
                    if it.exists(-2):
                        pe.wait_ge(y_ready, it.unit(-1))
                        if it.layer(-2) == CAUSAL:
                            pe.wait_ge(placing, it.batch(-2) * len(PLACING) + 2)
                    pe.wait_ge(xt_sb, it.unit(2))
                    for t in range(NT):
                        last = nc.tensor.matmul(misc[1][:, t * C:(t + 1) * C], x_t[:, t * P:(t + 1) * P],
                                                wq_sb[it.layer(1)][:, 2 * C:3 * C], start=True, stop=True)
                    last.then_inc(v_ps, 1)
                if it.exists(-1):
                    for t in range(NT):
                        if f"t{t}" not in jobs:
                            continue
                        if t == 0:
                            pe.wait_ge(o_copied, it.unit(0) * GROUPS)
                        if t >= 2:
                            pe.wait_ge(on_ready, it.unit(-1) * NT + (t - 1))
                        elif it.layer_now == LOCAL:
                            pe.wait_ge(rest_ready[1 - t], it.unit(3))
                        elif t == 0:
                            pe.wait_ge(lo_ready, it.unit(1) if it.exists(0) else UNITS)
                        elif it.exists(1):
                            pe.wait_ge(v_ready, it.unit(2))
                        else:
                            pe.wait_ge(placing, it.batch(-2) * len(PLACING) + 2)
                        for g in range(GROUPS):
                            last = nc.tensor.transpose(misc[t % 2][:, g * P:(g + 1) * P], o_t[it.slot(-1)][:, g, t * P:(t + 1) * P], ident[:, :])
                        last.then_inc(ot_ps, 1)
                if "on" in jobs and it.exists(-1):
                    pe.wait_ge(on_ready, it.unit(0) * NT)
                    for t in range(NT):
                        last = nc.tensor.transpose(misc[0][:, t * P:(t + 1) * P], o_norm[:, t, :], ident[:, :])
                    last.then_inc(ont_ps, 1)
                if "out" in jobs and it.exists(-1):
                    pe.wait_ge(ont_sb, it.unit(0))
                    for t in range(NT):
                        last = nc.tensor.matmul(misc[1][:, t * C:(t + 1) * C], o_norm_t[:, t * P:(t + 1) * P],
                                                wo_sb[it.layer(-1)][:, :], start=True, stop=True)
                    last.then_inc(proj_ps, 1)
                if "xt" in jobs and it.exists(2):
                    p = it.slot(2)
                    if it.layer(2) == LOCAL:
                        pe.wait_ge(h_loaded[p], (it.same_parity_before(2) + 1) * 16)
                    else:
                        pe.wait_ge(h_ready, it.batch(3))
                    if it.layer_now == CAUSAL:
                        pe.wait_ge(ont_sb, it.unit(0))
                    elif it.exists(0):
                        pe.wait_ge(lo_ready, it.unit(1))
                    elif it.exists(1):
                        pe.wait_ge(rest_ready[1], it.unit(2))
                    for t in range(NT):
                        last = nc.tensor.transpose(misc[0][:, t * P:(t + 1) * P], h_in[p][:, t, :], ident[:, :])
                    last.then_inc(xt_ps, 1)
                if "qk" in jobs and it.exists(2):
                    pe.wait_ge(xt_sb, it.unit(3))
                    if it.layer_now == CAUSAL:
                        pe.wait_ge(y_ready, it.unit(0))
                    elif it.exists(1):
                        pe.wait_ge(v_ready, it.unit(2))
                    w = wq_sb[it.layer(2)]
                    nc.tensor.matmul(misc[1][:, :], w[:, 0:C], x_t[:, :], start=True, stop=True).then_inc(q_ps, 1)
                    nc.tensor.matmul(misc[0][:, :], w[:, C:2 * C], x_t[:, :], start=True, stop=True).then_inc(k_ps, 1)
                if it.exists(-1) and it.layer(-1) == CAUSAL:
                    if "xf" in jobs:
                        pe.wait_ge(moe_in_ready, it.batch(0))
                        if it.exists(2):
                            pe.wait_ge(rest_ready[0], it.unit(3))
                        for t in range(NT):
                            last = nc.tensor.transpose(misc[1][:, t * P:(t + 1) * P], rows[:, 0, t, 0:C], ident[:, :])
                        last.then_inc(xf_ps, 1)
                    if "route" in jobs:
                        pe.wait_ge(xf_sb, it.batch(0))
                        for t in range(NT):
                            last = nc.tensor.matmul(misc[1][:, t * E:(t + 1) * E], moe_in_t[:, t * P:(t + 1) * P], wg_sb[:, :],
                                                    start=True, stop=True)
                        last.then_inc(logits_ps, 1)
                    if "rank" in jobs:
                        pe.wait_ge(routed, it.batch(-1) * len(ROUTE) + 5)
                        width = CHOICES + 1
                        for d in range(width):
                            shifted = onehot[:, CHOICES - d:CHOICES - d + width, :].rearrange("p n e -> p (n e)")
                            last = nc.tensor.matmul(misc[1][:, 0:width * E], square_b[:, :] if d else tri_b[:, :], shifted,
                                                    start=(d == 0), stop=(d == CHOICES))
                        last.then_inc(ranked, 1)
                if "shift" in jobs and it.exists(1):
                    pe.wait_ge(max_taken, banks_before(it, 2))
                    if it.exists(-1):
                        pe.wait_ge(ont_sb, it.unit(0))
                    if it.exists(2):
                        pe.wait_ge(rest_ready[1], it.unit(3))
                    for i in range(NT):
                        last = nc.tensor.transpose(misc[0][0:H, i * P:(i + 1) * P], row_max[it.slot(1)][:, i, :], ident[:, :])
                    last.then_inc(maxt_ps, 1)

            def iteration(it):
                for k in range(it.steps):
                    banks = it.banks_at(k)

                    first = [(len(banks) * part + 3) // 4 for part in range(5)]

                    def maxima(part):
                        for n in banks[first[part]:first[part + 1]]:
                            max_bank(it, n)

                    for c in range(GROUP):
                        if it.exists(0):
                            score_chunk(it, k, c)
                        if c == 0 and it.layer_now == LOCAL:
                            side_jobs(it, k)
                        maxima(c)
                        if c == 2:
                            if k == 0 and it.exists(-1):
                                times_v(it, -1, STEPS[it.layer(-1)] - 1)
                            elif k > 0 and it.exists(0):
                                times_v(it, 0, k - 1)
                    if it.layer_now == CAUSAL:
                        side_jobs(it, k)

            run(pe, iteration)
            pe.wait_ge(exp_done, CHUNKS_ALL)
            pe.wait_ge(max_taken, BANKS_ALL)
            pe.wait_ge(o_copied, UNITS * GROUPS)
            pe.wait_ge(ont_sb, UNITS)
            pe.wait_ge(placing, B * len(PLACING))

            def stage(m, like, turn):
                if 1 <= like <= BLOCKS:
                    n, i, w = m - 1, (like - 1) % 2, (like - 1) % W_DEPTH
                    pe.wait_ge(w_in[w], loads(turn, like, 1, W_DEPTH) * 16)
                    pe.wait_ge(bx_sb, n + 1)
                    if like >= 3:
                        pe.wait_ge(hidden_ready, (n - 1) * FT)
                    for f in range(FT):
                        last = nc.tensor.matmul(hidden_ps[2 * i + f // 2][:, f % 2 * BLK:(f % 2 + 1) * BLK],
                                                block_w[w][:, PACK_W1 + f * P:PACK_W1 + (f + 1) * P], block_xt[i],
                                                start=True, stop=True)
                        if f % 2 == 1:
                            last.then_inc(hidden_filled, 1)
                if like < BLOCKS:
                    pe.wait_ge(x_in[like % DEPTH], loads(turn, like, 0) * 16)
                    if like >= 2:
                        pe.wait_ge(bx_sb, m - 1)
                    for t in range(BLT):
                        last = nc.tensor.transpose(misc[like % 2][:, t * P:(t + 1) * P], block_x[like % DEPTH][:, t, 0:C], ident[:, :])
                    last.then_inc(bx_ps, 1)
                if like >= 2:
                    n, i, w = m - 2, like % 2, (like - 2) % W_DEPTH
                    pe.wait_ge(hidden_ready, (n + 1) * FT)
                    if like >= 4:
                        pe.wait_ge(biased, n - 1)
                    for t in range(BLT):
                        for f in range(FT):
                            last = nc.tensor.matmul(y_ps[i][:, t * C:(t + 1) * C], hidden[:, i * FT + f, t * P:(t + 1) * P],
                                                    block_w[w][:, PACK_W2 + f * C:PACK_W2 + (f + 1) * C],
                                                    start=(f == 0), stop=(f == FT - 1))
                    last.then_inc(block_ps, 1)

            run_blocks(pe, stage)


INPUTS = ["L0_attn_x", "L0_attn_w_qkv", "L0_attn_w_out", "L0_ffn_ln1_g", "L0_ffn_ln1_b", "L0_ffn_ln2_g", "L0_ffn_ln2_b",
          "L0_ffn_w_qkv", "L0_ffn_w_o", "L0_ffn_w_gate", "L0_ffn_w1", "L0_ffn_b1", "L0_ffn_w2", "L0_ffn_b2"]


def kernel(**inputs):
    import concourse.bacc as bacc
    from concourse.bass_utils import run_bass_kernel_spmd

    nc = bacc.Bacc("TRN2", target_bir_lowering=False, num_devices=1)
    arrays, args = {}, []
    for name in INPUTS:
        a = np.ascontiguousarray(inputs[name])
        arrays[f"in_{name}"] = a
        args.append(nc.dram_tensor(f"in_{name}", a.shape, mybir.dt.from_np(a.dtype), kind="ExternalInput").ap())
    args.append(nc.dram_tensor("out_x", (B, T, C), F32, kind="ExternalOutput").ap())
    build(nc, *args)
    r = run_bass_kernel_spmd(nc, [arrays], core_ids=[0])
    return r.results[0]["out_x"]
```
